# Optimizing a Trainium2 kernel written in Bass

```python
import numpy as np
import jax
import jax.numpy as jnp

def _softmax(x, axis=-1):
    return jax.nn.softmax(x, axis=axis)

def _gelu(x):
    return jax.nn.gelu(x, approximate=True)

def _silu(x):
    return jax.nn.silu(x)

def _sigmoid(x):
    return jax.nn.sigmoid(x)

def _layernorm(x, axis=-1, eps=1e-05):
    m = jnp.mean(x, axis=axis, keepdims=True)
    v = jnp.var(x, axis=axis, keepdims=True)
    return (x - m) / jnp.sqrt(v + eps)

def _scatter_add(tgt, idx, src, axis=0):
    return tgt.at[idx].add(src)

def _segment_sum(src, seg, n):
    return jax.ops.segment_sum(src, seg, n)
kernel_name = 'mk_sandwich_d1_jaxref_r4_0ccf14'

def setup_inputs(seed: int=0):
    np.random.seed(seed)
    _w = jnp.asarray

    def _L0_attn_setup():
        import jax, jax.numpy as jnp
        import numpy as np
        HIDDEN = 256
        NUM_HEAD = 16
        HEAD_DIM = HIDDEN // NUM_HEAD
        B, S = (2, 512)
        key = jax.random.key(seed)
        ks = jax.random.split(key, 9)
        std = 1.0 / np.sqrt(HIDDEN)
        x = jax.random.normal(ks[0], (B, S, HIDDEN), dtype=jnp.float32)
        Wq = jax.random.normal(ks[1], (HIDDEN, HIDDEN), dtype=jnp.float32) * std
        Wk = jax.random.normal(ks[2], (HIDDEN, HIDDEN), dtype=jnp.float32) * std
        Wv = jax.random.normal(ks[3], (HIDDEN, HIDDEN), dtype=jnp.float32) * std
        Wo = jax.random.normal(ks[4], (HIDDEN, HIDDEN), dtype=jnp.float32) * std
        bq = jax.random.normal(ks[5], (HIDDEN,), dtype=jnp.float32) * std
        bk = jax.random.normal(ks[6], (HIDDEN,), dtype=jnp.float32) * std
        bv = jax.random.normal(ks[7], (HIDDEN,), dtype=jnp.float32) * std
        bo = jax.random.normal(ks[8], (HIDDEN,), dtype=jnp.float32) * std
        return {'x': x, 'Wq': Wq, 'bq': bq, 'Wk': Wk, 'bk': bk, 'Wv': Wv, 'bv': bv, 'Wo': Wo, 'bo': bo}
    _L0_attn_in = _L0_attn_setup()

    def _L0_ffn_setup():
        import jax, jax.numpy as jnp
        import numpy as np
        HIDDEN = 256
        INTER = 1024
        key = jax.random.key(seed)
        k1, k2, k3, k4, k5 = jax.random.split(key, 5)
        hidden_states = jax.random.normal(k1, (4, 512, HIDDEN), dtype=jnp.float32)
        W1 = jax.random.normal(k2, (HIDDEN, INTER), dtype=jnp.float32) * (1.0 / np.sqrt(HIDDEN))
        b1 = jax.random.normal(k3, (INTER,), dtype=jnp.float32) * 0.02
        W2 = jax.random.normal(k4, (INTER, HIDDEN), dtype=jnp.float32) * (1.0 / np.sqrt(INTER))
        b2 = jax.random.normal(k5, (HIDDEN,), dtype=jnp.float32) * 0.02
        return {'hidden_states': hidden_states, 'W1': W1, 'b1': b1, 'W2': W2, 'b2': b2}
    _L0_ffn_in = _L0_ffn_setup()
    _d = {'L0_attn_x': _L0_attn_in['x'], 'L0_attn_Wq': _L0_attn_in['Wq'], 'L0_attn_bq': _L0_attn_in['bq'], 'L0_attn_Wk': _L0_attn_in['Wk'], 'L0_attn_bk': _L0_attn_in['bk'], 'L0_attn_Wv': _L0_attn_in['Wv'], 'L0_attn_bv': _L0_attn_in['bv'], 'L0_attn_Wo': _L0_attn_in['Wo'], 'L0_attn_bo': _L0_attn_in['bo'], 'L0_ffn_W1': _L0_ffn_in['W1'], 'L0_ffn_b1': _L0_ffn_in['b1'], 'L0_ffn_W2': _L0_ffn_in['W2'], 'L0_ffn_b2': _L0_ffn_in['b2']}
    _x0 = _d['L0_attn_x']
    _d['L0_attn_x'] = jax.random.normal(jax.random.fold_in(jax.random.key(seed), 1), (1, 4096, 256), dtype=_x0.dtype)
    del _x0
    return _d

def reference(L0_attn_x, L0_attn_Wq, L0_attn_bq, L0_attn_Wk, L0_attn_bk, L0_attn_Wv, L0_attn_bv, L0_attn_Wo, L0_attn_bo, L0_ffn_W1, L0_ffn_b1, L0_ffn_W2, L0_ffn_b2):

    def _L0_attn_ref(x, Wq, bq, Wk, bk, Wv, bv, Wo, bo):
        import jax, jax.numpy as jnp
        import numpy as np
        HIDDEN = 256
        NUM_HEAD = 16
        HEAD_DIM = HIDDEN // NUM_HEAD
        B, S = (2, 512)
        b, s, _ = x.shape

        def proj(W, bias):
            return (x @ W + bias).reshape(b, s, NUM_HEAD, HEAD_DIM).transpose(0, 2, 1, 3)
        q, k, v = (proj(Wq, bq), proj(Wk, bk), proj(Wv, bv))
        scale = 1.0 / np.sqrt(HEAD_DIM).astype(np.float32)
        scores = jnp.einsum('bhqd,bhkd->bhqk', q, k) * scale
        causal = jnp.tril(jnp.ones((s, s), dtype=bool))
        scores = jnp.where(causal[None, None], scores, jnp.float32(-100000.0))
        attn = jax.nn.softmax(scores, axis=-1)
        out = jnp.einsum('bhqk,bhkd->bhqd', attn, v)
        out = out.transpose(0, 2, 1, 3).reshape(b, s, NUM_HEAD * HEAD_DIM)
        return out @ Wo + bo

    def _L0_ffn_ref(hidden_states, W1, b1, W2, b2):
        import jax, jax.numpy as jnp
        import numpy as np
        HIDDEN = 256
        INTER = 1024
        h = jax.nn.relu(jnp.einsum('bsh,hi->bsi', hidden_states, W1) + b1)
        return jnp.einsum('bsi,ih->bsh', h, W2) + b2
    x = L0_attn_x
    x = x + _layernorm(_L0_attn_ref(_layernorm(x, axis=-1), L0_attn_Wq, L0_attn_bq, L0_attn_Wk, L0_attn_bk, L0_attn_Wv, L0_attn_bv, L0_attn_Wo, L0_attn_bo), axis=-1)
    x = x + _layernorm(_L0_ffn_ref(_layernorm(x, axis=-1), L0_ffn_W1, L0_ffn_b1, L0_ffn_W2, L0_ffn_b2), axis=-1)
    return x

_drawn_inputs = setup_inputs


def setup_inputs(seed=0):
    import zlib

    import numpy as np

    out = dict(_drawn_inputs(seed))
    spreads = {}
    factors = {'L0_attn_bk': 8.0, 'L0_ffn_b1': 4.787, 'L0_ffn_b2': 3.454}
    for name, (base, spread) in spreads.items():
        noise = np.random.default_rng([zlib.crc32(name.encode()), seed]).standard_normal(out[name].shape)
        drawn = base * np.exp(spread * noise) if base else spread * noise
        out[name] = jnp.asarray(drawn.astype(out[name].dtype))
    for name, factor in factors.items():
        out[name] = (out[name] * factor).astype(out[name].dtype)
    return out
```

```python
import concourse.bass as bass
from concourse import mybir
from contextlib import ExitStack



def sandwich_block_kernel(nc, x, Wq, bq, Wk, bk, Wv, bv, Wo, bo, W1, b1, W2, b2, out):
    fp32, bf16 = mybir.dt.float32, mybir.dt.bfloat16
    ALU, ACT, AX = mybir.AluOpType, mybir.ActivationFunctionType, mybir.AxisListType

    P = 128
    _, S, D = x.shape
    F = W1.shape[1]
    H = 16
    HD = D // H
    SCALE = float(HD) ** -0.5
    EPS = 1e-5
    NEG = -1e30
    CH = 512
    C = S // CH
    T = S // P
    TC = CH // P
    KD = D // P
    KF = F // P

    PARTS = 3
    PAIRS = 6 * HD
    AUG = PAIRS + 2

    QUADS = [(c, jq) for c in range(C) for jq in range(c + 1)]
    NQ = len(QUADS)
    LAST_QUAD = {s for s, (c, jq) in enumerate(QUADS) if jq == c}
    UNITS = [(i, u) for i in range(T) for u in range(i // TC + 1)]
    assert len(UNITS) == 4 * NQ
    LEAD = 12
    HEADS_IN_BODY = 2
    STEPS = HEADS_IN_BODY * NQ
    SLOTS = sum((i // TC + 2) // 2 for i in range(T))
    assert SLOTS % 2 == 0
    QUADS_IN_RING = 3
    RING = 4 * QUADS_IN_RING
    EXP_BANKS, MAX_SLOTS, H_BANKS = 2, 2, 2
    STACK_DMAS = 9
    VH_STEP = 8

    def slot_of(i, u):
        return sum((t // TC + 2) // 2 for t in range(i)) + u // 2

    def last_of_slot(i, u):
        return u % 2 == 1 or u == i // TC

    def max_units(step):
        g = (step + LEAD) % STEPS
        return [((g // NQ), *UNITS[4 * (g % NQ) + k]) for k in range(4)]

    def chunk_maxed(step):
        done = [(hb, i // TC) for hb, i, u in max_units(step) if i % TC == TC - 1 and u == i // TC]
        return done[0] if done else None

    EARLY = [(i, u) for i, u in UNITS[:4 * LEAD]]
    SLOTS_EARLY = sum(last_of_slot(i, u) for i, u in EARLY)
    CHUNKS_EARLY = sum(i % TC == TC - 1 and u == i // TC for i, u in EARLY)

    def misc_uses():
        uses = []
        for st in range(STEPS):
            if chunk_maxed((st - 1) % STEPS):
                uses.append("shift")
            if st >= 2 and (st - 2) % NQ in LAST_QUAD:
                uses.append("sums")
        return uses + ["sums"]

    SHIFT_USES = [n + 1 for n, kind in enumerate(misc_uses()) if kind == "shift"]

    def exp_cols(c, j):
        return max(0, (j - TC * c)) * P

    ctx = ExitStack()
    with ctx:
        def sb(name, shape, dt=fp32):
            return ctx.enter_context(nc.sbuf_tensor(name, shape, dt))

        def sem(name):
            return ctx.enter_context(nc.semaphore(name))

        identf = sb("identf", [P, P])
        identb = sb("identb", [P, P], bf16)
        causal_neg = sb("causal_neg", [P, P], bf16)
        eps_t = sb("eps_t", [P, 1])
        x_sb = sb("x_sb", [P, T, D])
        v_sb = sb("v_sb", [P, T, D])
        attn_sb = sb("attn_sb", [P, T, D])
        wqkv = attn_sb[:, 0:3 * KD, :].rearrange("p (w k) n -> p w k n", w=3)
        bq_t = sb("bq_t", [P, KD])
        bqs_t = sb("bqs_t", [P, KD])
        bk_t = sb("bk_t", [P, KD])
        bv_b = sb("bv_b", [P, 2, D])
        wo_t = sb("wo_t", [P, KD, D])
        bo_b = sb("bo_b", [P, 2, D])
        b2_b = sb("b2_b", [P, 2, D])
        b1_t = sb("b1_t", [P, KF])
        xn = sb("xn", [P, TC, D])
        xnT = sb("xnT", [P, 2, KD, CH])
        st6 = sb("st6", [P, TC, 6])
        mv = sb("mv", [P, TC, 2])
        std = sb("std", [P, TC])
        rstd = sb("rstd", [P, TC])
        qs = [sb(f"qs{b}", [AUG, S], bf16) for b in range(2)]
        ks = [sb(f"ks{b}", [AUG, S], bf16) for b in range(2)]
        vh = [sb(f"vh{b}", [P, T, 32]) for b in range(2)]
        prob = sb("prob", [P, RING, CH])
        qf, rf = prob[:, 0:2, :], prob[:, 2:4, :]
        parts = prob[:, 4:7, :].rearrange("p a n -> p (a n)").bitcast(bf16).rearrange(
            "p (b s n) -> p b s n", b=2, s=PARTS)
        mx = sb("mx", [P, 2, TC, 4])
        negm = sb("negm", [P, 2, TC])
        shift = sb("shift", [TC, 2, 2, P], bf16)
        acc_s = sb("acc_s", [P, 2, CH])
        osum = sb("osum", [P, 2, TC, HD + 1])
        rden = sb("rden", [P, 2, TC])
        w1_t = sb("w1_t", [P, KD, F])
        w2_t = sb("w2_t", [P, KF, D])
        hT = prob[:, 0:KF, :]
        attn_c = xn
        rowT = xnT[:, 0]
        xn2T = xnT[:, 1]
        y, xn2, y2 = (v_sb[:, n * TC:(n + 1) * TC, :] for n in range(3))

        ps = [ctx.enter_context(nc.psum_tensor(f"ps{i}", [P, 2, CH], fp32)) for i in range(4)]

        def bank(n):
            return ps[n // 2][:, n % 2, :]

        EXP_BANK, ACC_BANK, MISC_BANK = 4, 6, 7

        scratch = nc.dram_tensor("qk_parts", [2, PARTS, D, S], bf16, kind="Internal").ap()

        const_ready = sem("const_ready")
        w_in = sem("w_in")
        w3_in = sem("w3_in")
        x_in = [sem(f"x_in{b}") for b in range(2)]
        bias_scaled = sem("bias_scaled")
        stats_ready = sem("stats_ready")
        std_ready = sem("std_ready")
        xn_ready = sem("xn_ready")
        xT_filled = sem("xT_filled")
        xT_copied = sem("xT_copied")
        qk_filled = sem("qk_filled")
        qk_evacuated = sem("qk_evacuated")
        qf_free = sem("qf_free")
        p2_ready = sem("p2_ready")
        parts_ready = sem("parts_ready")
        parts_stored = [sem(f"parts_stored{b}") for b in range(2)]
        v_filled = sem("v_filled")
        v_evacuated = sem("v_evacuated")
        dve1 = sem("dve1")
        stack_in = [sem(f"stack_in{b}") for b in range(2)]
        vh_ready = sem("vh_ready")
        slot_filled = sem("slot_filled")
        slot_reduced = sem("slot_reduced")
        negm_ready = sem("negm_ready")
        misc_filled = sem("misc_filled")
        misc_read = sem("misc_read")
        shift_hi = sem("shift_hi")
        shift_in = [sem(f"shift_in{b}") for b in range(2)]
        scores_filled = sem("scores_filled")
        exp_done = sem("exp_done")
        mask_done = sem("mask_done")
        pv_done = sem("pv_done")
        acc_copied = sem("acc_copied")
        rden_ready = sem("rden_ready")
        attn_written = sem("attn_written")
        attn_c_ready = sem("attn_c_ready")
        t3_filled = sem("t3_filled")
        t3_copied = sem("t3_copied")
        y_filled = sem("y_filled")
        y_evacuated = sem("y_evacuated")
        stats3 = sem("stats3")
        std3 = sem("std3")
        xn2_ready = sem("xn2_ready")
        h_filled = sem("h_filled")
        h_ready = sem("h_ready")
        y2_filled = sem("y2_filled")
        y2_evacuated = sem("y2_evacuated")
        dve3 = sem("dve3")
        out_ready = sem("out_ready")
        out_stored = sem("out_stored")

        def wait_apart(eng, s, value):
            value = value if isinstance(value, int) else eng.to_reg(value)
            eng.wait_ge(const_ready, CONSTS)
            eng.wait_ge(s, value)

        def linker(eng, s, base):
            n = [0]

            def link(ins, apart=False):
                n[0] += 1
                ins.then_inc(s, 1)
                if apart:
                    wait_apart(eng, s, base + n[0])
                else:
                    eng.wait_ge(s, base + n[0])

            return link

        def tiles(t, c, n=TC):
            return t[:, bass.ds(c * TC, n), :]

        x_v = x.rearrange("o (t p) d -> p (o t) d", p=P)
        out_v = out.rearrange("o (t p) d -> p (o t) d", p=P)

        CONSTS = 13
        LOADS = 7
        LOADS3 = 8
        SPLITS = 2 * KD
        LN1_LINKS, SPLIT_LINKS = 2, SPLITS
        LN3_LINKS, FINISH_LINKS = 6, 3
        block = ctx.enter_context(nc.Block())

        @block.sync
        def _(sp):
            def load_x(c, b):
                sp.dma_start(tiles(x_sb, c), tiles(x_v, c)).then_inc(x_in[b], 16)

            def store_parts(c):
                for n in range(SPLITS):
                    sp.wait_ge(parts_ready, c * SPLITS + n + 1)
                    dst = scratch[n // KD, :, (n % KD) * P:(n % KD + 1) * P, bass.ds(c * CH, CH)]
                    sp.dma_start(dst.rearrange("s p n -> p s n"), parts[:, n % 2]).then_inc(parts_stored[n % 2], 16)

            load_x(0, 0)
            load_x(1, 1)
            with sp.Fori(0, C // 2 - 1) as it:
                for b in range(2):
                    sp.wait_ge(x_in[b], (it + 1) * 16)
                    load_x(it * 2 + b + 2, b)
                    store_parts(it * 2 + b)
            for c in (C - 2, C - 1):
                store_parts(c)

            for b in range(2):
                sp.wait_ge(parts_stored[b], C * SPLITS // 2 * 16)

            def load_stack(h, b):
                row = 0
                for n in (3, 2, 1):
                    part = 3 - n
                    qsrc = scratch[0, 0:n, bass.ds(h * HD, HD), :]
                    sp.dma_start(qs[b][row:row + n * HD, :], qsrc).then_inc(stack_in[b], 16)
                    for r in range(n):
                        ksrc = scratch[1, part, bass.ds(h * HD, HD), :]
                        sp.dma_start(ks[b][row + r * HD:row + (r + 1) * HD, :], ksrc).then_inc(stack_in[b], 16)
                    row += n * HD

            def send_shift(n, hb, c):
                sp.wait_ge(misc_read, n)
                dst = qs[hb][PAIRS:AUG, c * CH:(c + 1) * CH].rearrange("s (t n) -> s t n", t=TC)
                for s in range(2):
                    sp.dma_start(dst[s:s + 1], shift[:, c % 2, s, :]).then_inc(shift_in[c % 2], 16)

            load_stack(0, 0)
            for n in range(CHUNKS_EARLY):
                send_shift(n + 1, 0, n)
            with sp.Fori(0, H // HEADS_IN_BODY) as it:
                uses = it * (2 * HEADS_IN_BODY * C) + CHUNKS_EARLY
                sent = 0
                for g in range(STEPS):
                    if g % NQ == 1:
                        hb = 1 - g // NQ
                        sp.wait_ge(exp_done, EXP_BANKS + it * (4 * STEPS) + 4 * NQ * (1 - hb))
                        load_stack((it * 2 + 1) if hb == 1 else (it * 2 + 2) % H, hb)
                    if chunk_maxed((g - 1) % STEPS):
                        send_shift(uses + SHIFT_USES[sent], *chunk_maxed((g - 1) % STEPS))
                        sent += 1

            with sp.Fori(0, C) as c:
                sp.wait_ge(out_ready, c + 1)
                sp.dma_start(tiles(out_v, c), y2[:, :, :]).then_inc(out_stored, 16)
            sp.wait_ge(out_stored, C * 16)
            for b in range(2):
                sp.wait_ge(shift_in[b], (H * C + CHUNKS_EARLY) // 2 * 32)
                sp.wait_ge(stack_in[b], (H // 2 + 1 - b) * STACK_DMAS * 16)

        @block.gpsimd
        def _(pool):
            g = nc.gpsimd
            made = [0]

            def constant(ins):
                made[0] += 1
                ins.then_inc(const_ready, 1)
                pool.wait_ge(const_ready, made[0])

            for m in (identf, identb, causal_neg):
                constant(g.memset(m[:, :], 0.0))
            constant(g.memset(eps_t[:, :], EPS))
            for m in (identf, identb):
                constant(g.affine_select(out=m[:, :], in_=m[:, :], compare_op=ALU.not_equal, fill=1.0, base=0,
                                         pattern=[[-1, P]], channel_multiplier=1))
            constant(g.affine_select(out=causal_neg[:, :], in_=causal_neg[:, :], compare_op=ALU.is_ge, fill=NEG,
                                     base=0, pattern=[[-1, P]], channel_multiplier=1))
            for b in range(2):
                constant(g.memset(ks[b][PAIRS:AUG, :], 1.0))
                constant(g.memset(vh[b][:, :, :], 0.0))
                constant(g.memset(vh[b][:, :, HD:HD + 1], 1.0))
            assert made[0] == CONSTS

            with pool.Fori(0, C) as c:
                for n in range(SPLITS):
                    pool.wait_ge(p2_ready, c * SPLITS + n + 1)
                    g.tensor_tensor(parts[:, n % 2, 2, :], rf[:, n % 2, :], parts[:, n % 2, 1, :],
                                    ALU.subtract).then_inc(parts_ready, 1)

            def lay_out_values(h, b):
                g.tensor_copy(vh[b][:, :, 0:HD], v_sb[:, :, bass.ds(h * HD, HD)]).then_inc(vh_ready, 1)

            pool.wait_ge(const_ready, CONSTS)
            pool.wait_ge(v_evacuated, 2 + 2 * C)
            lay_out_values(0, 0)

            def scale_out(n, c, h):
                pool.wait_ge(rden_ready, n)
                g.tensor_tensor(attn_sb[:, c * TC:(c + 1) * TC, bass.ds(h * HD, HD)],
                                osum[:, c % 2, :, 0:HD],
                                rden[:, c % 2, :].unsqueeze(2).broadcast_to([P, TC, HD]),
                                ALU.mult).then_inc(attn_written, 1)

            with pool.Fori(0, H // HEADS_IN_BODY) as it:
                quads = it * STEPS
                masks = it * (HEADS_IN_BODY * C * 4)
                chunks = it * (HEADS_IN_BODY * C)
                masked = ended = 0
                for st in range(STEPS):
                    hb, (c, jq) = st // NQ, QUADS[st % NQ]
                    if st % NQ == VH_STEP:
                        pool.wait_ge(pv_done, QUADS_IN_RING + quads + NQ * hb)
                        lay_out_values((it * 2 + 1) if hb == 0 else (it * 2 + 2) % H, 1 - hb)
                    if st % NQ in LAST_QUAD:
                        for k in range(4):
                            slot = (4 * st + k) % RING
                            wait_apart(pool, exp_done, EXP_BANKS + quads * 4 + 4 * st + k + 1)
                            if c == 0 and k > 0:
                                g.memset(prob[:, slot, 0:k * P], 0.0)
                            g.affine_select(out=prob[:, slot, k * P:(k + 1) * P],
                                            in_=prob[:, slot, k * P:(k + 1) * P],
                                            compare_op=ALU.is_ge, fill=0.0, base=0,
                                            pattern=[[1, P]], channel_multiplier=-1).then_inc(mask_done, 1)
                            masked += 1
                    if st >= 3 and (st - 3) % NQ in LAST_QUAD:
                        ended += 1
                        scale_out(chunks + ended, QUADS[(st - 3) % NQ][0], it * 2 + (st - 3) // NQ)
                ended += 1
                scale_out(chunks + ended, C - 1, it * 2 + 1)

            pool.wait_ge(attn_written, 2 + H * C)
            g.tensor_copy(attn_c[:, :, :], tiles(attn_sb, 0)).then_inc(attn_c_ready, 1)
            with pool.Fori(0, C - 1) as c:
                pool.wait_ge(t3_filled, c * 4 + 2)
                g.tensor_copy(attn_c[:, :, :], tiles(attn_sb, c + 1)).then_inc(attn_c_ready, 1)

        @block.scalar
        def _(act):
            for n, w in enumerate((Wq, Wk, Wv)):
                act.dma_start(wqkv[:, n], w.rearrange("(k p) n -> p k n", p=P)).then_inc(w_in, 16)
            act.dma_start(bq_t[:, :], bq.rearrange("(m p) -> p m", p=P), allow_slow_non_contiguous=True).then_inc(w_in, 16)
            act.dma_start(bk_t[:, :], bk.rearrange("(m p) -> p m", p=P), allow_slow_non_contiguous=True).then_inc(w_in, 16)

            def load_bias_rows(dst, src, s):
                for r in range(2):
                    act.dma_start(dst[:, r, :], src.partition_broadcast(P)).then_inc(s, 16)

            load_bias_rows(bv_b, bv, w_in)
            act.dma_start(wo_t[:, :, :], Wo.rearrange("(k p) n -> p k n", p=P)).then_inc(w3_in, 16)
            load_bias_rows(bo_b, bo, w3_in)
            load_bias_rows(b2_b, b2, w3_in)
            act.dma_start(b1_t[:, :], b1.rearrange("(m p) -> p m", p=P), allow_slow_non_contiguous=True).then_inc(w3_in, 16)
            act.dma_start(w1_t[:, :, :], W1.rearrange("(k p) n -> p k n", p=P)).then_inc(w3_in, 16)
            act.dma_start(w2_t[:, :, :], W2.rearrange("(k p) n -> p k n", p=P)).then_inc(w3_in, 16)

            def deviation(c):
                act.wait_ge(stats_ready, c + 1)
                nc.scalar.activation(std[:, :], mv[:, :, 1], ACT.Sqrt, bias=eps_t[:, 0:1]).then_inc(std_ready, 1)

            def copy_xT(c, b):
                for k in range(KD):
                    act.wait_ge(xT_filled, c * KD + k + 1)
                    nc.scalar.activation(xnT[:, b, k, :], bank(k), ACT.Copy).then_inc(xT_copied, 1)

            def evacuate_qk(c):
                for n in range(SPLITS):
                    act.wait_ge(qk_filled, c * SPLITS + n + 1)
                    act.wait_ge(qf_free, c * SPLITS + n + 1)
                    bias = (bqs_t, bk_t)[n // KD][:, n % KD:n % KD + 1]
                    nc.scalar.activation(qf[:, n % 2, :], bank(2 + n), ACT.Identity, bias=bias,
                                         scale=(SCALE, 1.0)[n // KD]).then_inc(qk_evacuated, 1)

            act.wait_ge(const_ready, CONSTS)
            act.wait_ge(w_in, LOADS * 16)
            act.wait_ge(bias_scaled, 1)
            deviation(0)
            copy_xT(0, 0)

            def chunk1(c, b, last=False):
                if not last:
                    deviation(c + 1)
                evacuate_qk(c)
                if not last:
                    copy_xT(c + 1, 1 - b)

            with act.Fori(0, C // 2 - 1) as it:
                for b in range(2):
                    chunk1(it * 2 + b, b)
            chunk1(C - 2, 0)
            chunk1(C - 1, 1, last=True)

            def copy_acc(c):
                nc.scalar.activation(acc_s[:, c % 2, :], bank(ACC_BANK), ACT.Copy).then_inc(acc_copied, 1)

            with act.Fori(0, H // HEADS_IN_BODY) as it:
                quads = it * STEPS
                chunks = it * (HEADS_IN_BODY * C)
                for st in range(STEPS):
                    c, jq = QUADS[st % NQ]
                    act.wait_ge(pv_done, quads + st + 1)
                    for k in range(4):
                        col = exp_cols(c, 4 * jq + k)
                        act.wait_ge(scores_filled, quads * 4 + 4 * st + k + 1)
                        nc.scalar.activation(prob[:, (4 * st + k) % RING, col:CH],
                                             bank(EXP_BANK + k % 2)[:, col:CH], ACT.Exp).then_inc(exp_done, 1)
                    if st > 0 and (st - 1) % NQ in LAST_QUAD:
                        act.wait_ge(pv_done, QUADS_IN_RING + quads + st)
                        copy_acc(QUADS[(st - 1) % NQ][0])
                act.wait_ge(pv_done, QUADS_IN_RING + quads + STEPS)
                copy_acc(C - 1)

            def copy_T3(c, k0, dst):
                for k in range(KD):
                    act.wait_ge(t3_filled, c * 4 + k0 + k + 1)
                    nc.scalar.activation(dst[:, k, :], bank(k), ACT.Copy).then_inc(t3_copied, 1)

            def deviation3(n):
                act.wait_ge(stats3, n)
                nc.scalar.activation(std[:, :], mv[:, :, 1], ACT.Sqrt, bias=eps_t[:, 0:1]).then_inc(std3, 1)

            def relu(c, f):
                act.wait_ge(h_filled, c * KF + f + 1)
                nc.scalar.activation(hT[:, f, :], bank(4 + f % 2), ACT.Relu,
                                     bias=b1_t[:, f:f + 1]).then_inc(h_ready, 1)

            act.wait_ge(w3_in, LOADS3 * 16)
            copy_T3(0, 0, rowT)
            deviation3(1)
            deviation3(2)
            copy_T3(0, 2, xn2T)
            with act.Fori(0, C - 1) as c:
                copy_T3(c + 1, 0, rowT)
                for f in range(0, 3):
                    relu(c, f)
                deviation3(c * 3 + 3)
                for f in range(3, 6):
                    relu(c, f)
                deviation3(c * 3 + 4)
                for f in range(6, KF):
                    relu(c, f)
                copy_T3(c + 1, 2, xn2T)
                deviation3(c * 3 + 5)
            for f in range(KF):
                relu(C - 1, f)
            deviation3(3 * C)

        @block.tensor
        def _(pe):
            mm, tr = nc.tensor.matmul, nc.tensor.transpose

            def transpose_x(c):
                pe.wait_ge(xn_ready, c + 1)
                pe.wait_ge(xT_copied, c * KD)
                for k in range(KD):
                    for t in range(TC):
                        last = tr(bank(k)[:, t * P:(t + 1) * P], xn[:, t, k * P:(k + 1) * P], identf[:, :])
                    last.then_inc(xT_filled, 1)

            def project_qk(c, b):
                pe.wait_ge(xT_copied, c * KD + KD)
                for n in range(SPLITS):
                    m = n % KD
                    pe.wait_ge(qk_evacuated, c * SPLITS + n + 1)
                    for k in range(KD):
                        last = mm(bank(2 + n), wqkv[:, n // KD, k, m * P:(m + 1) * P], xnT[:, b, k, :],
                                  start=(k == 0), stop=(k == KD - 1))
                    last.then_inc(qk_filled, 1)

            def project_v(c, b):
                for h in range(2):
                    pe.wait_ge(v_evacuated, c * 2 + h + 1)
                    for t in (2 * h, 2 * h + 1):
                        for k in range(KD):
                            last = mm(bank(6 + h)[:, (t % 2) * D:(t % 2 + 1) * D], xnT[:, b, k, t * P:(t + 1) * P],
                                      wqkv[:, 2, k, :], start=(k == 0), stop=(k == KD - 1))
                    last.then_inc(v_filled, 1)

            def chunk1(c, b, last=False):
                project_qk(c, b)
                if not last:
                    transpose_x(c + 1)
                project_v(c, b)

            pe.sem_inc(qk_evacuated, SPLITS)
            pe.sem_inc(qf_free, 2)
            pe.sem_inc(v_evacuated, 2)
            pe.wait_ge(const_ready, CONSTS)
            pe.wait_ge(w_in, LOADS * 16)
            transpose_x(0)
            with pe.Fori(0, C // 2 - 1) as it:
                for b in range(2):
                    chunk1(it * 2 + b, b)
            chunk1(C - 2, 0)
            chunk1(C - 1, 1, last=True)

            def score_max(n, hb, i, u):
                c, slot = i // TC, slot_of(i, u) % 2
                cols = CH if u < c else (i % TC + 1) * P
                if u % 2 == 0:
                    pe.wait_ge(slot_reduced, n)
                dst = ps[slot][:, u % 2, :]
                diag = u == c
                last = mm(dst[:, 0:cols], qs[hb][0:PAIRS, i * P:(i + 1) * P], ks[hb][0:PAIRS, u * CH:u * CH + cols],
                          start=True, stop=not diag)
                if diag:
                    last = mm(dst[:, cols - P:cols], identb[:, :], causal_neg[:, :], start=False, stop=True)
                if last_of_slot(i, u):
                    last.then_inc(slot_filled, 1)

            def turn_shift(n, uses, c):
                pe.wait_ge(negm_ready, n)
                pe.wait_ge(misc_read, uses)
                tr(bank(MISC_BANK)[0:TC, 0:P], negm[:, c % 2, :], identf[:, :]).then_inc(misc_filled, 1)

            def turn_sums(n, uses, c):
                pe.wait_ge(acc_copied, n)
                pe.wait_ge(misc_read, uses)
                for t in range(TC):
                    last = tr(bank(MISC_BANK)[:, t * P:(t + 1) * P], acc_s[:, c % 2, t * P:(t + 1) * P], identf[:, :])
                last.then_inc(misc_filled, 1)

            def values(st, quads, masks, chunks):
                hb, (c, jq) = st // NQ, QUADS[st % NQ]
                if jq == 0:
                    pe.wait_ge(acc_copied, chunks + hb * C + c)
                if c == 0:
                    pe.wait_ge(vh_ready, vh_base + hb + 1)
                pe.wait_ge(exp_done, EXP_BANKS + quads * 4 + 4 * st + 4)
                if jq == c:
                    pe.wait_ge(mask_done, masks + 4 * (hb * C + c + 1))
                for k in range(4):
                    j = 4 * jq + k
                    col = exp_cols(c, j) if c else 0
                    last = mm(bank(ACC_BANK)[32 * k:32 * k + 32, col:CH], vh[hb][:, j, :],
                              prob[:, (4 * st + k) % RING, col:CH], start=(jq == 0), stop=(jq == c))
                last.then_inc(pv_done, 1)

            pe.sem_inc(exp_done, EXP_BANKS)
            pe.sem_inc(pv_done, QUADS_IN_RING)
            pe.sem_inc(slot_reduced, MAX_SLOTS)
            pe.sem_inc(attn_written, 2)
            pe.wait_ge(qk_evacuated, SPLITS + C * SPLITS)
            pe.wait_ge(v_evacuated, 2 + 2 * C)
            pe.wait_ge(xT_copied, KD * C)
            pe.wait_ge(stack_in[0], STACK_DMAS * 16)
            slots = uses = turned = 0
            for g in range(LEAD):
                for k in range(4):
                    i, u = UNITS[4 * g + k]
                    score_max(slot_of(i, u) + 1, 0, i, u)
                if g > 0 and chunk_maxed((g - 1 - LEAD) % STEPS):
                    turned += 1
                    turn_shift(turned, uses, turned - 1)
                    uses += 1
            assert turned == CHUNKS_EARLY
            with pe.Fori(0, H // HEADS_IN_BODY) as it:
                quads = it * STEPS
                masks = it * (HEADS_IN_BODY * C * 4)
                chunks = it * (HEADS_IN_BODY * C)
                vh_base = it * 2
                uses0 = it * (2 * HEADS_IN_BODY * C) + CHUNKS_EARLY
                turned0 = it * (HEADS_IN_BODY * C) + CHUNKS_EARLY
                slots0 = it * (HEADS_IN_BODY * SLOTS)
                uses = turned = summed = 0
                for st in range(STEPS):
                    hb, (c, jq) = st // NQ, QUADS[st % NQ]
                    if jq == 0:
                        pe.wait_ge(shift_in[c % 2], (it * C + hb * (C // 2) + c // 2 + 1) * 32)
                    for k, (mb, i, u) in enumerate(max_units(st)):
                        col = exp_cols(c, 4 * jq + k)
                        pe.wait_ge(exp_done, quads * 4 + 4 * st + k + 1)
                        mm(bank(EXP_BANK + k % 2)[:, col:CH], ks[hb][0:AUG, (4 * jq + k) * P:(4 * jq + k + 1) * P],
                           qs[hb][0:AUG, c * CH + col:(c + 1) * CH], start=True, stop=True).then_inc(scores_filled, 1)
                        if (i, u) == (0, 0):
                            head = (it + 1) if mb == 0 else it
                            pe.wait_ge(stack_in[mb], (head + 1) * (STACK_DMAS * 16))
                        wrap = HEADS_IN_BODY if (st + LEAD >= STEPS) else mb
                        score_max(slots0 + (wrap * SLOTS + slot_of(i, u) + 1), mb, i, u)
                        if k == 1 and chunk_maxed((st - 1) % STEPS):
                            turned += 1
                            turn_shift(turned0 + turned, uses0 + uses, chunk_maxed((st - 1) % STEPS)[1])
                            uses += 1
                    if st >= 2 and (st - 2) % NQ in LAST_QUAD:
                        summed += 1
                        turn_sums(chunks + summed, uses0 + uses, QUADS[(st - 2) % NQ][0])
                        uses += 1
                    if st >= 1:
                        values(st - 1, quads, masks, chunks)
                values(STEPS - 1, quads, masks, chunks)
                summed += 1
                turn_sums(chunks + summed, uses0 + uses, C - 1)
                uses += 1
                assert uses == 2 * HEADS_IN_BODY * C and turned == summed

            def attend_out(c):
                pe.wait_ge(attn_c_ready, c + 1)
                pe.wait_ge(t3_copied, c * 4)
                for k in range(KD):
                    for t in range(TC):
                        last = tr(bank(k)[:, t * P:(t + 1) * P], attn_c[:, t, k * P:(k + 1) * P], identf[:, :])
                    last.then_inc(t3_filled, 1)
                pe.wait_ge(t3_copied, c * 4 + KD)
                pe.wait_ge(y_evacuated, c * 2 + 2)
                for t in range(TC):
                    for k in range(KD):
                        last = mm(bank(2 + t // 2)[:, (t % 2) * D:(t % 2 + 1) * D], rowT[:, k, t * P:(t + 1) * P],
                                  wo_t[:, k, :], start=(k == 0), stop=(k == KD - 1))
                    if t % 2:
                        last.then_inc(y_filled, 1)

            def transpose_xn2(c):
                pe.wait_ge(xn2_ready, c + 1)
                pe.wait_ge(t3_copied, c * 4 + KD)
                for k in range(KD):
                    for t in range(TC):
                        last = tr(bank(k)[:, t * P:(t + 1) * P], xn2[:, t, k * P:(k + 1) * P], identf[:, :])
                    last.then_inc(t3_filled, 1)

            def ffn(c):
                pe.wait_ge(t3_copied, c * 4 + 4)
                for f in range(KF):
                    pe.wait_ge(h_ready, c * KF + f + 1)
                    for k in range(KD):
                        last = mm(bank(4 + f % 2), w1_t[:, k, f * P:(f + 1) * P], xn2T[:, k, :],
                                  start=(k == 0), stop=(k == KD - 1))
                    last.then_inc(h_filled, 1)
                pe.wait_ge(y2_evacuated, c * 2 + 2)
                for t in range(TC):
                    for f in range(KF):
                        if t == 0:
                            pe.wait_ge(h_ready, H_BANKS + c * KF + f + 1)
                        last = mm(bank(6 + t // 2)[:, (t % 2) * D:(t % 2 + 1) * D], hT[:, f, t * P:(t + 1) * P],
                                  w2_t[:, f, :], start=(f == 0), stop=(f == KF - 1))
                    if t % 2:
                        last.then_inc(y2_filled, 1)

            pe.sem_inc(h_ready, H_BANKS)
            pe.sem_inc(y_evacuated, 2)
            pe.sem_inc(y2_evacuated, 2)
            pe.wait_ge(w3_in, LOADS3 * 16)
            pe.wait_ge(misc_read, 2 * H * C + CHUNKS_EARLY)
            pe.wait_ge(slot_reduced, MAX_SLOTS + H * SLOTS + SLOTS_EARLY)
            attend_out(0)
            transpose_xn2(0)
            with pe.Fori(0, C - 1) as c:
                attend_out(c + 1)
                ffn(c)
                transpose_xn2(c + 1)
            ffn(C - 1)

        @block.vector
        def _(dve):
            v = nc.vector

            def statistics(src, link):
                for t in range(TC):
                    last = v.bn_stats(st6[:, t, :], src(t))
                link(last, apart=True)
                for t in range(TC):
                    last = v.bn_aggr(mv[:, t, :], st6[:, t, :])
                return last

            def normalise(dst, src, t):
                return v.tensor_scalar(dst, src, mv[:, t, 0:1], rstd[:, t:t + 1], ALU.subtract, ALU.mult)

            def layer_norm1(c, b, loads, links):
                link = linker(dve, dve1, links)
                wait_apart(dve, x_in[b], loads * 16)
                statistics(lambda t: x_sb[:, bass.ds(c * TC + t, 1), :], link).then_inc(stats_ready, 1)
                dve.wait_ge(std_ready, c + 1)
                link(v.reciprocal(rstd[:, :], std[:, :]))
                dve.wait_ge(xT_filled, c * KD)
                for t in range(TC):
                    last = normalise(xn[:, t, :], x_sb[:, bass.ds(c * TC + t, 1), :], t)
                last.then_inc(xn_ready, 1)

            def split(c, links):
                link = linker(dve, dve1, links)
                for n in range(SPLITS):
                    s = n % 2
                    dve.wait_ge(qk_evacuated, SPLITS + c * SPLITS + n + 1)
                    dve.wait_ge(parts_stored[s], (c * (SPLITS // 2) + n // 2) * 16)
                    link(v.tensor_copy(parts[:, s, 0, :], qf[:, s, :]))
                    v.tensor_tensor(rf[:, s, :], qf[:, s, :], parts[:, s, 0, :], ALU.subtract).then_inc(qf_free, 1)
                    dve.wait_ge(qf_free, 2 + c * SPLITS + n + 1)
                    v.tensor_copy(parts[:, s, 1, :], rf[:, s, :]).then_inc(p2_ready, 1)

            def add_v_bias(c):
                for h in range(2):
                    dve.wait_ge(v_filled, c * 2 + h + 1)
                    v.tensor_tensor(v_sb[:, bass.ds(c * TC + 2 * h, 2), :],
                                    bank(6 + h).rearrange("p (t n) -> p t n", t=2), bv_b[:, :, :],
                                    ALU.add).then_inc(v_evacuated, 1)

            def chunk1(c, b, it, last=False):
                links = c * (LN1_LINKS + SPLIT_LINKS) + LN1_LINKS
                if not last:
                    layer_norm1(c + 1, 1 - b, it + 1 + b, links)
                split(c, links if last else links + LN1_LINKS)
                add_v_bias(c)

            dve.wait_ge(w_in, LOADS * 16)
            v.tensor_scalar(bqs_t[:, :], bq_t[:, :], SCALE, None, ALU.mult).then_inc(bias_scaled, 1)
            layer_norm1(0, 0, 1, 0)
            with dve.Fori(0, C // 2 - 1) as it:
                for b in range(2):
                    chunk1(it * 2 + b, b, it)
            chunk1(C - 2, 0, C // 2 - 1)
            chunk1(C - 1, 1, C // 2 - 1, last=True)

            def row_max(n, i, u, finals):
                c, slot = i // TC, slot_of(i, u) % 2
                if i % TC == 0 and u <= 1:
                    dve.wait_ge(negm_ready, finals)
                width = (u % 2) * CH + (CH if u < c else (i % TC + 1) * P)
                dve.wait_ge(slot_filled, n)
                v.tensor_reduce(mx[:, c % 2, i % TC, u // 2:u // 2 + 1],
                                ps[slot][:, :, :].rearrange("p a n -> p (a n)")[:, 0:width],
                                axis=AX.X, op=ALU.max).then_inc(slot_reduced, 1)

            def chunk_max(n, c):
                dve.wait_ge(slot_reduced, MAX_SLOTS + n)
                v.tensor_reduce(negm[:, c % 2, :], mx[:, c % 2, :, 0:(c + 2) // 2], axis=AX.X, op=ALU.max,
                                negate=True).then_inc(negm_ready, 1)

            def split_shift(use, n, c):
                dve.wait_ge(misc_filled, use)
                dve.wait_ge(shift_in[c % 2], n)
                v.tensor_copy(shift[:, c % 2, 0, :], bank(MISC_BANK)[0:TC, 0:P]).then_inc(shift_hi, 1)

            def shift_low(use, n, c):
                dve.wait_ge(shift_hi, n)
                v.tensor_tensor(shift[:, c % 2, 1, :], bank(MISC_BANK)[0:TC, 0:P], shift[:, c % 2, 0, :],
                                ALU.subtract).then_inc(misc_read, 1)

            def add_sums(use, n, c):
                dve.wait_ge(misc_filled, use)
                dve.wait_ge(attn_written, n)
                sums = bank(MISC_BANK).rearrange("p (t k d) -> p t d k", t=TC, k=4)
                v.tensor_reduce(osum[:, c % 2, :, :], sums[:, :, 0:HD + 1, :], axis=AX.X,
                                op=ALU.add).then_inc(misc_read, 1)
                dve.wait_ge(misc_read, use)
                v.reciprocal(rden[:, c % 2, :], osum[:, c % 2, :, HD]).then_inc(rden_ready, 1)

            uses = 0
            for g in range(LEAD):
                for k in range(4):
                    i, u = UNITS[4 * g + k]
                    if last_of_slot(i, u):
                        row_max(slot_of(i, u) + 1, i, u, i // TC)
                        if i % TC == TC - 1 and u == i // TC:
                            chunk_max(slot_of(i, u) + 1, i // TC)
                    if k == 1 and g > 0 and chunk_maxed((g - 1 - LEAD) % STEPS):
                        uses += 1
                        split_shift(uses, (uses - 1) // 2 * 32, uses - 1)
                        shift_low(uses, uses, uses - 1)
            with dve.Fori(0, H // HEADS_IN_BODY) as it:
                chunks = it * (HEADS_IN_BODY * C)
                uses0 = it * (2 * HEADS_IN_BODY * C) + CHUNKS_EARLY
                slots0 = it * (HEADS_IN_BODY * SLOTS)
                uses = turned = summed = 0
                for st in range(STEPS):
                    for k, (mb, i, u) in enumerate(max_units(st)):
                        wrap = HEADS_IN_BODY if st + LEAD >= STEPS else mb
                        if last_of_slot(i, u):
                            row_max(slots0 + (wrap * SLOTS + slot_of(i, u) + 1), i, u, chunks + wrap * C + i // TC)
                            if i % TC == TC - 1 and u == i // TC:
                                chunk_max(slots0 + (wrap * SLOTS + slot_of(i, u) + 1), i // TC)
                        if k == 1 and chunk_maxed((st - 1) % STEPS):
                            uses += 1
                            turned += 1
                            c = chunk_maxed((st - 1) % STEPS)[1]
                            before = it * (HEADS_IN_BODY * C * 16) + (CHUNKS_EARLY + turned - 1) // 2 * 32
                            split_shift(uses0 + uses, before, c)
                            shift_low(uses0 + uses, chunks + (CHUNKS_EARLY + turned), c)
                    if st >= 2 and (st - 2) % NQ in LAST_QUAD:
                        uses += 1
                        summed += 1
                        add_sums(uses0 + uses, chunks + summed, QUADS[(st - 2) % NQ][0])
                uses += 1
                summed += 1
                add_sums(uses0 + uses, chunks + summed, C - 1)

            def add_bias3(bank0, bias, dst, filled, evacuated, c):
                for h in range(2):
                    dve.wait_ge(filled, c * 2 + h + 1)
                    v.tensor_tensor(dst[:, 2 * h:2 * h + 2, :], bank(bank0 + h).rearrange("p (t n) -> p t n", t=2),
                                    bias[:, :, :], ALU.add).then_inc(evacuated, 1)
                wait_apart(dve, evacuated, 2 + c * 2 + 2)

            def standard3(src, link, n):
                statistics(src, link).then_inc(stats3, 1)
                dve.wait_ge(std3, n)
                link(v.reciprocal(rstd[:, :], std[:, :]))

            def attention_branch(c, norms, links):
                link = linker(dve, dve3, links)
                add_bias3(2, bo_b, y, y_filled, y_evacuated, c)
                standard3(lambda t: y[:, t, :], link, norms + 1)
                for t in range(TC):
                    last = normalise(y[:, t, :], y[:, t, :], t)
                link(last)
                link(v.tensor_tensor(tiles(x_sb, c), tiles(x_sb, c), y[:, :, :], ALU.add), apart=True)
                standard3(lambda t: x_sb[:, bass.ds(c * TC + t, 1), :], link, norms + 2)
                for t in range(TC):
                    last = normalise(xn2[:, t, :], x_sb[:, bass.ds(c * TC + t, 1), :], t)
                last.then_inc(xn2_ready, 1)

            def finish(c, norms, links):
                link = linker(dve, dve3, links)
                dve.wait_ge(out_stored, c * 16)
                add_bias3(6, b2_b, y2, y2_filled, y2_evacuated, c)
                standard3(lambda t: y2[:, t, :], link, norms + 1)
                for t in range(TC):
                    last = normalise(y2[:, t, :], y2[:, t, :], t)
                link(last)
                v.tensor_tensor(y2[:, :, :], y2[:, :, :], tiles(x_sb, c), ALU.add).then_inc(out_ready, 1)

            dve.wait_ge(w3_in, LOADS3 * 16)
            attention_branch(0, 0, 0)
            with dve.Fori(0, C - 1) as c:
                links = c * (LN3_LINKS + FINISH_LINKS) + LN3_LINKS
                attention_branch(c + 1, c * 3 + 2, links)
                finish(c, c * 3 + 4, links + LN3_LINKS)
            finish(C - 1, 3 * C - 1, (C - 1) * (LN3_LINKS + FINISH_LINKS) + LN3_LINKS)


_INS = ["x", "Wq", "bq", "Wk", "bk", "Wv", "bv", "Wo", "bo", "W1", "b1", "W2", "b2"]
_NAMES = [f"L0_attn_{n}" for n in _INS[:9]] + [f"L0_ffn_{n}" for n in _INS[9:]]


def kernel(**inputs):
    import numpy as _np
    import concourse.bacc as _bacc
    from concourse import mybir as _mybir
    from concourse.bass_utils import run_bass_kernel_spmd as _run

    nc = _bacc.Bacc("TRN2", target_bir_lowering=False, num_devices=1)
    arrays, args = {}, []
    for name in _NAMES:
        a = _np.ascontiguousarray(inputs[name])
        arrays[f"in_{name}"] = a
        args.append(nc.dram_tensor(f"in_{name}", a.shape, _mybir.dt.from_np(a.dtype), kind="ExternalInput").ap())
    out = nc.dram_tensor("out_dram", arrays["in_L0_attn_x"].shape, _mybir.dt.float32, kind="ExternalOutput").ap()
    sandwich_block_kernel(nc, *args, out)
    r = _run(nc, [arrays], core_ids=[0])
    return r.results[0]["out_dram"]
```

```python
import concourse.bass as bass
from concourse import mybir
from contextlib import ExitStack



def sandwich_block_kernel(nc, x, Wq, bq, Wk, bk, Wv, bv, Wo, bo, W1, b1, W2, b2, out):
    fp32, bf16 = mybir.dt.float32, mybir.dt.bfloat16
    ALU, ACT, AX = mybir.AluOpType, mybir.ActivationFunctionType, mybir.AxisListType

    P = 128
    _, S, D = x.shape
    F = W1.shape[1]
    H = 16
    HD = D // H
    SCALE = float(HD) ** -0.5
    EPS = 1e-5
    NEG = -1e30
    CH = 512
    C = S // CH
    T = S // P
    TC = CH // P
    KD = D // P
    KF = F // P

    PARTS = 3
    PAIRS = 6 * HD
    AUG = PAIRS + 2

    QUADS = [(c, jq) for c in range(C) for jq in range(c + 1)]
    NQ = len(QUADS)
    ENTRIES = [(i, list(range(u, min(u + 2, i // TC + 1)))) for i in range(T) for u in range(0, i // TC + 1, 2)]
    LEAD = 11
    LEAD_SLACK = 2
    EARLY_COUNT = [sum(len(us) for _, us in ENTRIES[:n]) for n in range(len(ENTRIES))].index(4 * LEAD)
    HEADS_IN_BODY = 2
    STEPS = HEADS_IN_BODY * NQ
    QUADS_IN_RING = 3
    RING = 4 * QUADS_IN_RING
    RING_BANKS = 5
    EXP_BANKS = 2
    ACC_BANK = RING_BANKS + EXP_BANKS
    H_BANKS = 2
    STACK_DMAS = 9
    VH_STEP = 22

    def exp_cols(c, j):
        return max(0, (j - TC * c)) * P

    def max_cols(i, u):
        return CH if u < i // TC else (i % TC + 1) * P

    class Plan:

        SYNC = 190
        NEAR = 60

        def __init__(self):
            self.pe = self.dve = self.act = self.pool = 0.0
            self.ring = [0.0] * RING_BANKS
            self.exp = [0.0] * EXP_BANKS
            self.acc = 0.0
            self.product = [0.0] * QUADS_IN_RING
            self.last = [0] * RING_BANKS

        def rested(self, n):
            return min(range(RING_BANKS - n + 1), key=lambda b: max(self.ring[b:b + n]))

        def enter(self, kind, at, n, *what):
            self.entries += 1
            need = max(self.last[at:at + n])
            self.last[at:at + n] = [self.entries] * n
            self.order.append((kind, self.entries, at, need, *what))

        def run(self, start, count, exp_side=True):
            self.order, self.entries = [], 0
            st = k = product = issued = 0
            units = 4 * LEAD if exp_side else 0
            turns, ready = [], {}
            while True:
                options = {}
                if exp_side and st < STEPS and st < product + QUADS_IN_RING and units >= 4 * (st + LEAD - LEAD_SLACK):
                    options["exp"] = self.exp[(4 * st + k) % EXP_BANKS]
                if issued < count and (not exp_side or units <= 4 * (min(st, STEPS - 1) + LEAD + LEAD_SLACK)):
                    hb, e = divmod(start + issued, len(ENTRIES))
                    i, us = ENTRIES[e]
                    at = self.rested(len(us))
                    options["max"] = max(self.ring[at:at + len(us)])
                if turns:
                    options[turns[0][0]] = max(turns[0][1], min(self.ring))
                if product < st:
                    c, jq = QUADS[product % NQ]
                    options["values"] = max(ready[product], self.acc if jq == 0 else 0)
                if not options:
                    return self.order
                usable = [x for x in ("shift", "sums", "exp", "max", "values")
                          if x in options and options[x] + self.SYNC <= self.pe + self.NEAR]
                if "values" in usable and st - product >= 2:
                    kind = "values"
                else:
                    kind = usable[0] if usable else min(options, key=options.get)
                self.pe = max(self.pe, options[kind] + self.SYNC)
                if kind == "exp":
                    c, jq = QUADS[st % NQ]
                    cols = CH - exp_cols(c, 4 * jq + k)
                    self.pe += cols / 2.4 + 3
                    if k == 0:
                        self.act = max(self.act, self.product[st % QUADS_IN_RING] + self.SYNC)
                    self.act = max(self.act, self.pe + self.SYNC) + cols / 1.2 + 52
                    self.exp[(4 * st + k) % EXP_BANKS] = ready[st] = self.act
                    if jq == c:
                        self.pool = ready[st] = max(self.pool, self.act + self.SYNC) + 244
                    self.order.append(("exp", st, k))
                    st, k = (st + 1, 0) if k == 3 else (st, k + 1)
                if kind == "max":
                    cols = sum(max_cols(i, u) for u in us)
                    self.pe += cols / 2.4 + 3 * len(us) + (56 if us[-1] == i // TC else 0)
                    self.dve = max(self.dve, self.pe + self.SYNC) + cols / 0.96 + 64
                    self.ring[at:at + len(us)] = [self.dve] * len(us)
                    self.enter("max", at, len(us), hb % HEADS_IN_BODY, i, us)
                    issued += 1
                    units += len(us)
                    if i % TC == TC - 1 and us[-1] == i // TC:
                        self.dve += self.SYNC + 85
                        turns.append(("shift", self.dve, hb % HEADS_IN_BODY, i // TC))
                if kind in ("shift", "sums"):
                    at = self.rested(1)
                    self.pe += {"shift": 107, "sums": 275}[kind]
                    self.dve = max(self.dve, self.pe + self.SYNC) + {"shift": 590, "sums": 348}[kind]
                    self.ring[at] = self.dve
                    self.dve += {"shift": 0, "sums": self.SYNC + 94}[kind]
                    self.enter(kind, at, 1, *turns.pop(0)[2:])
                if kind == "values":
                    self.pe += 4 * (320 if jq == c and c else CH) / 2.4 + 61
                    self.product[product % QUADS_IN_RING] = self.pe
                    self.order.append(("values", product))
                    product += 1
                    if jq == c:
                        self.acc = self.act = max(self.act, self.pe + self.SYNC) + 478
                        self.order.append(("copy", c))
                        turns.append(("sums", self.acc, c))

    plan = Plan()
    EARLY = plan.run(0, EARLY_COUNT, exp_side=False)
    EARLY_ENTRIES = plan.entries
    before = [n - EARLY_ENTRIES for n in plan.last]
    for settling in range(4):
        plan.last = list(before)
        BODY = plan.run(EARLY_COUNT, HEADS_IN_BODY * len(ENTRIES))
        BODY_ENTRIES = plan.entries
        before = [max(b, n - BODY_ENTRIES) for b, n in zip(before, plan.last)]
    assert all(b >= n - BODY_ENTRIES for b, n in zip(before, plan.last))
    EARLY_CHUNKS = sum(x[0] == "shift" for x in EARLY)

    ctx = ExitStack()
    with ctx:
        def sb(name, shape, dt=fp32):
            return ctx.enter_context(nc.sbuf_tensor(name, shape, dt))

        def sem(name):
            return ctx.enter_context(nc.semaphore(name))

        identf = sb("identf", [P, P])
        identb = sb("identb", [P, P], bf16)
        causal_neg = sb("causal_neg", [P, P], bf16)
        eps_t = sb("eps_t", [P, 1])
        x_sb = sb("x_sb", [P, T, D])
        v_sb = sb("v_sb", [P, T, D])
        attn_sb = sb("attn_sb", [P, T, D])
        wqkv = attn_sb[:, 0:3 * KD, :].rearrange("p (w k) n -> p w k n", w=3)
        bq_t = sb("bq_t", [P, KD])
        bqs_t = sb("bqs_t", [P, KD])
        bk_t = sb("bk_t", [P, KD])
        bv_b = sb("bv_b", [P, 2, D])
        wo_t = sb("wo_t", [P, KD, D])
        bo_b = sb("bo_b", [P, 2, D])
        b2_b = sb("b2_b", [P, 2, D])
        b1_t = sb("b1_t", [P, KF])
        xn = sb("xn", [P, TC, D])
        xnT = sb("xnT", [P, 2, KD, CH])
        st6 = sb("st6", [P, TC, 6])
        mv = sb("mv", [P, TC, 2])
        std = sb("std", [P, TC])
        rstd = sb("rstd", [P, TC])
        qs = [sb(f"qs{b}", [AUG, S], bf16) for b in range(2)]
        ks = [sb(f"ks{b}", [AUG, S], bf16) for b in range(2)]
        vh = [sb(f"vh{b}", [P, T, 32]) for b in range(2)]
        prob = sb("prob", [P, RING, CH])
        SPLITS = 2 * KD
        qf, rf = prob[:, 0:SPLITS, :], prob[:, SPLITS:SPLITS + 2, :]
        parts = prob[:, SPLITS + 2:SPLITS + 2 + SPLITS * PARTS // 2, :].rearrange("p a n -> p (a n)").bitcast(
            bf16).rearrange("p (b s n) -> p b s n", b=SPLITS, s=PARTS)
        mx = sb("mx", [P, 2, TC, 4])
        negm = sb("negm", [P, 2, TC])
        shift = sb("shift", [TC, 2, 2, P], bf16)
        acc_s = sb("acc_s", [P, 2, CH])
        osum = sb("osum", [P, 2, TC, HD + 1])
        rden = sb("rden", [P, 2, TC])
        w1_t = sb("w1_t", [P, KD, F])
        w2_t = sb("w2_t", [P, KF, D])
        hT = prob[:, 0:KF, :]
        attn_c = xn
        rowT = xnT[:, 0]
        xn2T = xnT[:, 1]
        y, xn2, y2 = (v_sb[:, n * TC:(n + 1) * TC, :] for n in range(3))

        ps = ctx.enter_context(nc.psum_tensor("ps", [P, 8, CH], fp32))

        def bank(n):
            return ps[:, n, :]

        EXP_BANK = RING_BANKS

        scratch = nc.dram_tensor("qk_parts", [2, PARTS, D, S], bf16, kind="Internal").ap()

        const_ready = sem("const_ready")
        w_in = sem("w_in")
        w3_in = sem("w3_in")
        x_in = [sem(f"x_in{b}") for b in range(2)]
        bias_scaled = sem("bias_scaled")
        stats_ready = sem("stats_ready")
        std_ready = sem("std_ready")
        xn_ready = sem("xn_ready")
        xT_filled = sem("xT_filled")
        xT_copied = sem("xT_copied")
        qk_filled = sem("qk_filled")
        qk_evacuated = sem("qk_evacuated")
        qf_free = sem("qf_free")
        p2_ready = sem("p2_ready")
        parts_ready = sem("parts_ready")
        parts_stored = [sem(f"parts_stored{n}") for n in range(SPLITS)]
        v_filled = sem("v_filled")
        v_evacuated = sem("v_evacuated")
        dve1 = sem("dve1")
        first_stack_in = sem("first_stack_in")
        stack_in = [sem(f"stack_in{b}") for b in range(2)]
        vh_ready = sem("vh_ready")
        ring_filled = sem("ring_filled")
        ring_read = sem("ring_read")
        negm_ready = sem("negm_ready")
        shift_hi = sem("shift_hi")
        shift_in = [sem(f"shift_in{b}") for b in range(2)]
        scores_filled = sem("scores_filled")
        exp_done = sem("exp_done")
        mask_done = sem("mask_done")
        pv_done = sem("pv_done")
        acc_copied = sem("acc_copied")
        rden_ready = sem("rden_ready")
        attn_written = sem("attn_written")
        attn_c_ready = sem("attn_c_ready")
        t3_filled = sem("t3_filled")
        t3_copied = sem("t3_copied")
        y_filled = sem("y_filled")
        y_evacuated = sem("y_evacuated")
        stats3 = sem("stats3")
        std3 = sem("std3")
        xn2_ready = sem("xn2_ready")
        h_filled = sem("h_filled")
        h_ready = sem("h_ready")
        y2_filled = sem("y2_filled")
        y2_evacuated = sem("y2_evacuated")
        dve3 = sem("dve3")
        out_ready = sem("out_ready")
        out_stored = sem("out_stored")

        def wait_apart(eng, s, value):
            value = value if isinstance(value, int) else eng.to_reg(value)
            eng.wait_ge(const_ready, FIRST_CONSTS)
            eng.wait_ge(s, value)

        def linker(eng, s, base):
            n = [0]

            def link(ins, apart=False):
                n[0] += 1
                ins.then_inc(s, 1)
                if apart:
                    wait_apart(eng, s, base + n[0])
                else:
                    eng.wait_ge(s, base + n[0])

            return link

        def tiles(t, c, n=TC):
            return t[:, bass.ds(c * TC, n), :]

        x_v = x.rearrange("o (t p) d -> p (o t) d", p=P)
        out_v = out.rearrange("o (t p) d -> p (o t) d", p=P)

        FIRST_CONSTS, CONSTS = 3, 13
        LOADS = 7
        LOADS3 = 8
        LN1_LINKS, SPLIT_LINKS = 2, SPLITS
        LN3_LINKS, FINISH_LINKS = 6, 3
        block = ctx.enter_context(nc.Block())

        @block.sync
        def _(sp):
            def load_x(c, b):
                sp.dma_start(tiles(x_sb, c), tiles(x_v, c)).then_inc(x_in[b], 16)

            def store_parts(c):
                for n in range(SPLITS):
                    sp.wait_ge(parts_ready, 2 + c * SPLITS + n + 1)
                    dst = scratch[n // KD, :, (n % KD) * P:(n % KD + 1) * P, bass.ds(c * CH, CH)]
                    sp.dma_start(dst.rearrange("s p n -> p s n"), parts[:, n]).then_inc(parts_stored[n], 16)

            load_x(0, 0)
            load_x(1, 1)
            with sp.Fori(0, C // 2 - 1) as it:
                for b in range(2):
                    sp.wait_ge(x_in[b], (it + 1) * 16)
                    load_x(it * 2 + b + 2, b)
                    store_parts(it * 2 + b)

            def load_stack(h, b, loaded, first=0, end=C):
                row, cols = 0, slice(first * CH, end * CH)
                for n in (3, 2, 1):
                    part = 3 - n
                    qsrc = scratch[0, 0:n, bass.ds(h * HD, HD), cols]
                    sp.dma_start(qs[b][row:row + n * HD, cols], qsrc).then_inc(loaded, 16)
                    for r in range(n):
                        ksrc = scratch[1, part, bass.ds(h * HD, HD), cols]
                        sp.dma_start(ks[b][row + r * HD:row + (r + 1) * HD, cols], ksrc).then_inc(loaded, 16)
                    row += n * HD

            def send_shift(n, hb, c):
                sp.wait_ge(ring_read, n)
                dst = qs[hb][PAIRS:AUG, c * CH:(c + 1) * CH].rearrange("s (t n) -> s t n", t=TC)
                for s in range(2):
                    sp.dma_start(dst[s:s + 1], shift[:, c % 2, s, :]).then_inc(shift_in[c % 2], 16)

            for first, end in ((0, C - 2), (C - 2, C)):
                for c in range(max(first, C - 2), end):
                    store_parts(c)
                for n in range(SPLITS):
                    sp.wait_ge(parts_stored[n], 16 + end * 16)
                load_stack(0, 0, stack_in[0] if first else first_stack_in, first, end)
            for what, entry, *rest in EARLY:
                if what == "shift":
                    send_shift(entry, *rest[2:])
            with sp.Fori(0, H // HEADS_IN_BODY) as it:
                entries = it * BODY_ENTRIES + EARLY_ENTRIES
                for what, *args in BODY:
                    if what == "exp" and args[0] % NQ == 1 and args[1] == 0:
                        hb = 1 - args[0] // NQ
                        sp.wait_ge(exp_done, EXP_BANKS + it * (4 * STEPS) + 4 * NQ * (1 - hb))
                        load_stack((it * 2 + 1) if hb == 1 else (it * 2 + 2) % H, hb, stack_in[hb])
                    if what == "shift":
                        entry, _, _, hb, c = args
                        send_shift(entries + entry, hb, c)

            with sp.Fori(0, C) as c:
                sp.wait_ge(out_ready, c + 1)
                sp.dma_start(tiles(out_v, c), y2[:, :, :]).then_inc(out_stored, 16)
            sp.wait_ge(out_stored, 16 + C * 16)
            for b in range(2):
                sp.wait_ge(shift_in[b], (H * C + EARLY_CHUNKS) // 2 * 32)
                sp.wait_ge(stack_in[b], (H // 2 + 1 - b) * STACK_DMAS * 16)

        @block.gpsimd
        def _(pool):
            g = nc.gpsimd
            made = [0]

            def constant(ins):
                made[0] += 1
                ins.then_inc(const_ready, 1)
                pool.wait_ge(const_ready, made[0])

            constant(g.memset(eps_t[:, :], EPS))
            for m in (identf, identb):
                constant(g.memset(m[:, :], 0.0))
                constant(g.affine_select(out=m[:, :], in_=m[:, :], compare_op=ALU.not_equal, fill=1.0, base=0,
                                         pattern=[[-1, P]], channel_multiplier=1))
            constant(g.memset(causal_neg[:, :], 0.0))
            constant(g.affine_select(out=causal_neg[:, :], in_=causal_neg[:, :], compare_op=ALU.is_ge, fill=NEG,
                                     base=0, pattern=[[-1, P]], channel_multiplier=1))
            for b in range(2):
                constant(g.memset(ks[b][PAIRS:AUG, :], 1.0))
                constant(g.memset(vh[b][:, :, :], 0.0))
                constant(g.memset(vh[b][:, :, HD:HD + 1], 1.0))
            assert made[0] == CONSTS

            with pool.Fori(0, C) as c:
                for n in range(SPLITS):
                    pool.wait_ge(p2_ready, c * SPLITS + n + 1)
                    g.tensor_tensor(parts[:, n, 2, :], rf[:, n % 2, :], parts[:, n, 1, :],
                                    ALU.subtract).then_inc(parts_ready, 1)

            def lay_out_values(h, b):
                g.tensor_copy(vh[b][:, :, 0:HD], v_sb[:, :, bass.ds(h * HD, HD)]).then_inc(vh_ready, 1)

            pool.wait_ge(const_ready, CONSTS)
            pool.wait_ge(v_evacuated, 2 + 2 * C)
            lay_out_values(0, 0)

            def scale_out(n, c, h):
                pool.wait_ge(rden_ready, n)
                g.tensor_tensor(attn_sb[:, c * TC:(c + 1) * TC, bass.ds(h * HD, HD)],
                                osum[:, c % 2, :, 0:HD],
                                rden[:, c % 2, :].unsqueeze(2).broadcast_to([P, TC, HD]),
                                ALU.mult).then_inc(attn_written, 1)

            def mask_diagonal(tiles_before, st, c):
                for k in range(4):
                    n = 4 * st + k
                    wait_apart(pool, exp_done, tiles_before + (EXP_BANKS + n + 1))
                    if c == 0 and k > 0:
                        g.memset(prob[:, n % RING, 0:k * P], 0.0)
                    g.affine_select(out=prob[:, n % RING, k * P:(k + 1) * P],
                                    in_=prob[:, n % RING, k * P:(k + 1) * P],
                                    compare_op=ALU.is_ge, fill=0.0, base=0,
                                    pattern=[[1, P]], channel_multiplier=-1).then_inc(mask_done, 1)

            with pool.Fori(0, H // HEADS_IN_BODY) as it:
                quads = it * STEPS
                chunks = it * (HEADS_IN_BODY * C)
                ended = 0
                for what, *args in BODY:
                    if what == "exp" and args[1] == 3:
                        st = args[0]
                        hb, (c, jq) = st // NQ, QUADS[st % NQ]
                        if st % NQ == VH_STEP:
                            pool.wait_ge(pv_done, QUADS_IN_RING + quads + NQ * hb)
                            lay_out_values((it * 2 + 1) if hb == 0 else (it * 2 + 2) % H, 1 - hb)
                        if jq == c:
                            mask_diagonal(quads * 4, st, c)
                    if what == "sums":
                        ended += 1
                        scale_out(chunks + ended, args[3], it * 2 + (ended - 1) // C)

            pool.wait_ge(attn_written, 2 + H * C)
            with pool.Fori(0, C - 2) as c:
                pool.wait_ge(t3_filled, c * 4 + 4)
                g.tensor_copy(attn_c[:, :, :], tiles(attn_sb, c + 2)).then_inc(attn_c_ready, 1)

        @block.scalar
        def _(act):
            for n, w in enumerate((Wq, Wk, Wv)):
                act.dma_start(wqkv[:, n], w.rearrange("(k p) n -> p k n", p=P)).then_inc(w_in, 16)
            act.dma_start(bq_t[:, :], bq.rearrange("(m p) -> p m", p=P), allow_slow_non_contiguous=True).then_inc(w_in, 16)
            act.dma_start(bk_t[:, :], bk.rearrange("(m p) -> p m", p=P), allow_slow_non_contiguous=True).then_inc(w_in, 16)

            def load_bias_rows(dst, src, s):
                for r in range(2):
                    act.dma_start(dst[:, r, :], src.partition_broadcast(P)).then_inc(s, 16)

            load_bias_rows(bv_b, bv, w_in)

            def deviation(c):
                act.wait_ge(stats_ready, c + 1)
                nc.scalar.activation(std[:, :], mv[:, :, 1], ACT.Sqrt, bias=eps_t[:, 0:1]).then_inc(std_ready, 1)

            def copy_xT(c, b):
                for k in range(KD):
                    act.wait_ge(xT_filled, c * KD + k + 1)
                    nc.scalar.activation(xnT[:, b, k, :], bank(k), ACT.Copy).then_inc(xT_copied, 1)

            def evacuate_qk(c):
                for n in range(SPLITS):
                    act.wait_ge(qk_filled, c * SPLITS + n + 1)
                    act.wait_ge(qf_free, c * SPLITS + n + 1)
                    bias = (bqs_t, bk_t)[n // KD][:, n % KD:n % KD + 1]
                    nc.scalar.activation(qf[:, n, :], bank(2 + n), ACT.Identity, bias=bias,
                                         scale=(SCALE, 1.0)[n // KD]).then_inc(qk_evacuated, 1)

            act.wait_ge(const_ready, FIRST_CONSTS)
            deviation(0)
            copy_xT(0, 0)
            act.dma_start(wo_t[:, :, :], Wo.rearrange("(k p) n -> p k n", p=P)).then_inc(w3_in, 16)
            load_bias_rows(bo_b, bo, w3_in)
            load_bias_rows(b2_b, b2, w3_in)
            act.dma_start(b1_t[:, :], b1.rearrange("(m p) -> p m", p=P), allow_slow_non_contiguous=True).then_inc(w3_in, 16)
            act.dma_start(w1_t[:, :, :], W1.rearrange("(k p) n -> p k n", p=P)).then_inc(w3_in, 16)
            act.dma_start(w2_t[:, :, :], W2.rearrange("(k p) n -> p k n", p=P)).then_inc(w3_in, 16)
            act.wait_ge(w_in, LOADS * 16)
            act.wait_ge(bias_scaled, 1)

            def chunk1(c, b, last=False):
                if not last:
                    deviation(c + 1)
                evacuate_qk(c)
                if not last:
                    copy_xT(c + 1, 1 - b)

            with act.Fori(0, C // 2 - 1) as it:
                for b in range(2):
                    chunk1(it * 2 + b, b)
            chunk1(C - 2, 0)
            chunk1(C - 1, 1, last=True)

            def copy_acc(c):
                nc.scalar.activation(acc_s[:, c % 2, :], bank(ACC_BANK), ACT.Copy).then_inc(acc_copied, 1)

            with act.Fori(0, H // HEADS_IN_BODY) as it:
                quads = it * STEPS
                for what, *args in BODY:
                    if what == "exp":
                        st, k = args
                        c, jq = QUADS[st % NQ]
                        if k == 0:
                            act.wait_ge(pv_done, quads + (st + 1))
                        col = exp_cols(c, 4 * jq + k)
                        act.wait_ge(scores_filled, quads * 4 + (4 * st + k + 1))
                        nc.scalar.activation(prob[:, (4 * st + k) % RING, col:CH],
                                             bank(EXP_BANK + (4 * st + k) % EXP_BANKS)[:, col:CH], ACT.Exp).then_inc(exp_done, 1)
                    if what == "values":
                        product = args[0]
                    if what == "copy":
                        act.wait_ge(pv_done, QUADS_IN_RING + quads + (product + 1))
                        copy_acc(args[0])

            def copy_T3(before, dst):
                for k in range(KD):
                    act.wait_ge(t3_filled, before + (k + 1))
                    nc.scalar.activation(dst[:, k, :], bank(k), ACT.Copy).then_inc(t3_copied, 1)

            def deviation3(n):
                act.wait_ge(stats3, n)
                nc.scalar.activation(std[:, :], mv[:, :, 1], ACT.Sqrt, bias=eps_t[:, 0:1]).then_inc(std3, 1)

            def relu(c, f):
                act.wait_ge(h_filled, c * KF + f + 1)
                nc.scalar.activation(hT[:, f, :], bank(4 + f % 2), ACT.Relu,
                                     bias=b1_t[:, f:f + 1]).then_inc(h_ready, 1)

            act.wait_ge(w3_in, LOADS3 * 16)
            copy_T3(0, rowT)
            copy_T3(KD, rowT)
            deviation3(1)
            deviation3(2)
            copy_T3(2 * KD, xn2T)

            def chunk3(c, last=False):
                for f in range(KF):
                    if f == 3:
                        deviation3(c * 3 + 3)
                    if f == 6:
                        deviation3(c * 3 + 4)
                    relu(c, f)
                if not last:
                    copy_T3(c * 4 + 6, rowT)
                copy_T3(c * 4 + (6 if last else 8), xn2T)
                deviation3(c * 3 + 5)

            with act.Fori(0, C - 2) as c:
                chunk3(c)
            chunk3(C - 2, last=True)
            for f in range(KF):
                relu(C - 1, f)
            deviation3(3 * C)

        @block.tensor
        def _(pe):
            mm, tr = nc.tensor.matmul, nc.tensor.transpose

            def transpose_x(c):
                pe.wait_ge(xn_ready, c + 1)
                if not (isinstance(c, int) and c == 0):
                    pe.wait_ge(xT_copied, c * KD)
                for k in range(KD):
                    for t in range(TC):
                        last = tr(bank(k)[:, t * P:(t + 1) * P], xn[:, t, k * P:(k + 1) * P], identf[:, :])
                    last.then_inc(xT_filled, 1)

            def project_qk(c, b):
                pe.wait_ge(xT_copied, c * KD + KD)
                for n in range(SPLITS):
                    m = n % KD
                    pe.wait_ge(qk_evacuated, c * SPLITS + n + 1)
                    for k in range(KD):
                        last = mm(bank(2 + n), wqkv[:, n // KD, k, m * P:(m + 1) * P], xnT[:, b, k, :],
                                  start=(k == 0), stop=(k == KD - 1))
                    last.then_inc(qk_filled, 1)

            def project_v(c, b):
                for h in range(2):
                    pe.wait_ge(v_evacuated, c * 2 + h + 1)
                    for t in (2 * h, 2 * h + 1):
                        for k in range(KD):
                            last = mm(bank(6 + h)[:, (t % 2) * D:(t % 2 + 1) * D], xnT[:, b, k, t * P:(t + 1) * P],
                                      wqkv[:, 2, k, :], start=(k == 0), stop=(k == KD - 1))
                    last.then_inc(v_filled, 1)

            def chunk1(c, b, last=False):
                project_qk(c, b)
                if not last:
                    transpose_x(c + 1)
                project_v(c, b)

            pe.sem_inc(qk_evacuated, SPLITS)
            pe.sem_inc(qf_free, SPLITS)
            pe.sem_inc(v_evacuated, 2)
            pe.wait_ge(const_ready, FIRST_CONSTS)
            transpose_x(0)
            pe.wait_ge(w_in, LOADS * 16)
            with pe.Fori(0, C // 2 - 1) as it:
                for b in range(2):
                    chunk1(it * 2 + b, b)
            chunk1(C - 2, 0)
            chunk1(C - 1, 1, last=True)

            def score_max(at, need, hb, i, us):
                if need is not None:
                    pe.wait_ge(ring_read, need)
                for u in us:
                    dst, cols, diag = bank(at + u - us[0]), max_cols(i, u), u == i // TC
                    last = mm(dst[:, 0:cols], qs[hb][0:PAIRS, i * P:(i + 1) * P], ks[hb][0:PAIRS, u * CH:u * CH + cols],
                              start=True, stop=not diag)
                    if diag:
                        last = mm(dst[:, cols - P:cols], identb[:, :], causal_neg[:, :], start=False, stop=True)
                last.then_inc(ring_filled, 1)

            def turn_shift(at, need, maxed, c):
                pe.wait_ge(negm_ready, maxed)
                pe.wait_ge(ring_read, need)
                tr(bank(at)[0:TC, 0:P], negm[:, c % 2, :], identf[:, :]).then_inc(ring_filled, 1)

            def turn_sums(at, need, copied, c):
                pe.wait_ge(acc_copied, 1 + copied)
                pe.wait_ge(ring_read, need)
                for t in range(TC):
                    last = tr(bank(at)[:, t * P:(t + 1) * P], acc_s[:, c % 2, t * P:(t + 1) * P], identf[:, :])
                last.then_inc(ring_filled, 1)

            def values(st, it):
                hb, (c, jq) = st // NQ, QUADS[st % NQ]
                if jq == 0:
                    pe.wait_ge(acc_copied, it * (HEADS_IN_BODY * C) + (hb * C + c + 1))
                if c == 0:
                    pe.wait_ge(vh_ready, it * HEADS_IN_BODY + (hb + 1))
                pe.wait_ge(exp_done, it * (4 * STEPS) + (EXP_BANKS + 4 * st + 4))
                if jq == c:
                    pe.wait_ge(mask_done, it * (HEADS_IN_BODY * C * 4) + 4 * (hb * C + c + 1))
                for k in range(4):
                    j = 4 * jq + k
                    col = exp_cols(c, j) if c else 0
                    last = mm(bank(ACC_BANK)[32 * k:32 * k + 32, col:CH], vh[hb][:, j, :],
                              prob[:, (4 * st + k) % RING, col:CH], start=(jq == 0), stop=(jq == c))
                last.then_inc(pv_done, 1)

            pe.sem_inc(exp_done, EXP_BANKS)
            pe.sem_inc(pv_done, QUADS_IN_RING)
            pe.sem_inc(acc_copied, 1)
            pe.sem_inc(attn_written, 2)
            pe.wait_ge(const_ready, CONSTS)
            pe.wait_ge(qk_evacuated, SPLITS + C * SPLITS)
            pe.wait_ge(v_evacuated, 2 + 2 * C)
            pe.wait_ge(xT_copied, KD * C)
            pe.wait_ge(first_stack_in, STACK_DMAS * 16)
            maxed = 0
            for what, _, at, need, *args in EARLY:
                if what == "max":
                    score_max(at, need if need > 0 else None, *args)
                if what == "shift":
                    maxed += 1
                    turn_shift(at, need, maxed, args[1])
            pe.wait_ge(stack_in[0], STACK_DMAS * 16)
            with pe.Fori(0, H // HEADS_IN_BODY) as it:
                entries = it * BODY_ENTRIES + EARLY_ENTRIES
                chunks = it * (HEADS_IN_BODY * C)
                maxed, copied = EARLY_CHUNKS, 0
                for what, *args in BODY:
                    if what == "exp":
                        st, k = args
                        hb, (c, jq) = st // NQ, QUADS[st % NQ]
                        if jq == 0 and k == 0:
                            pe.wait_ge(shift_in[c % 2], (it * C + (hb * (C // 2) + c // 2 + 1)) * 32)
                        j, col = 4 * jq + k, exp_cols(c, 4 * jq + k)
                        pe.wait_ge(exp_done, it * (4 * STEPS) + (4 * st + k + 1))
                        mm(bank(EXP_BANK + (4 * st + k) % EXP_BANKS)[:, col:CH], ks[hb][0:AUG, j * P:(j + 1) * P],
                           qs[hb][0:AUG, c * CH + col:(c + 1) * CH], start=True, stop=True).then_inc(scores_filled, 1)
                    if what == "max":
                        _, at, need, hb, i, us = args
                        if (i, us[0]) == (0, 0):
                            pe.wait_ge(stack_in[hb], (it + 2 - hb) * (STACK_DMAS * 16))
                        score_max(at, entries + need, hb, i, us)
                    if what == "shift":
                        maxed += 1
                        _, at, need, hb, c = args
                        turn_shift(at, entries + need, chunks + maxed, c)
                    if what == "sums":
                        copied += 1
                        _, at, need, c = args
                        turn_sums(at, entries + need, chunks + copied, c)
                    if what == "values":
                        values(args[0], it)

            def turn(src):
                for k in range(KD):
                    for t in range(TC):
                        last = tr(bank(k)[:, t * P:(t + 1) * P], src[:, t, k * P:(k + 1) * P], identf[:, :])
                    last.then_inc(t3_filled, 1)

            def attend_out(c):
                pe.wait_ge(t3_copied, c * 4 if not isinstance(c, int) or c else KD)
                pe.wait_ge(y_evacuated, c * 2 + 2)
                for t in range(TC):
                    for k in range(KD):
                        last = mm(bank(2 + t // 2)[:, (t % 2) * D:(t % 2 + 1) * D], rowT[:, k, t * P:(t + 1) * P],
                                  wo_t[:, k, :], start=(k == 0), stop=(k == KD - 1))
                    if t % 2:
                        last.then_inc(y_filled, 1)

            def ffn_up(c, copied):
                pe.wait_ge(t3_copied, copied)
                for f in range(KF):
                    pe.wait_ge(h_ready, c * KF + f + 1)
                    for k in range(KD):
                        last = mm(bank(4 + f % 2), w1_t[:, k, f * P:(f + 1) * P], xn2T[:, k, :],
                                  start=(k == 0), stop=(k == KD - 1))
                    last.then_inc(h_filled, 1)

            def ffn_down(c, h):
                pe.wait_ge(y2_evacuated, c * 2 + h + 1)
                for t in (2 * h, 2 * h + 1):
                    for f in range(KF):
                        if t == 0:
                            pe.wait_ge(h_ready, H_BANKS + c * KF + f + 1)
                        last = mm(bank(6 + h)[:, (t % 2) * D:(t % 2 + 1) * D], hT[:, f, t * P:(t + 1) * P],
                                  w2_t[:, f, :], start=(f == 0), stop=(f == KF - 1))
                last.then_inc(y2_filled, 1)

            def chunk3(c, last=False):
                attend_out(c + 1)
                ffn_up(c, c * 4 + 6)
                if not last:
                    pe.wait_ge(attn_c_ready, c + 1)
                    turn(attn_c)
                ffn_down(c, 0)
                pe.wait_ge(xn2_ready, c + 2)
                pe.wait_ge(t3_copied, c * 4 + (6 if last else 8))
                turn(xn2)
                ffn_down(c, 1)

            pe.sem_inc(h_ready, H_BANKS)
            pe.sem_inc(y_evacuated, 2)
            pe.sem_inc(y2_evacuated, 2)
            pe.wait_ge(w3_in, LOADS3 * 16)
            pe.wait_ge(ring_read, H // HEADS_IN_BODY * BODY_ENTRIES + EARLY_ENTRIES)
            pe.wait_ge(attn_written, 2 + (H - 1) * C + 2)
            turn(attn_sb[:, 0:TC, :])
            attend_out(0)
            turn(attn_sb[:, TC:2 * TC, :])
            pe.wait_ge(xn2_ready, 1)
            pe.wait_ge(t3_copied, 2 * KD)
            turn(xn2)
            with pe.Fori(0, C - 2) as c:
                chunk3(c)
            chunk3(C - 2, last=True)
            ffn_up(C - 1, 4 * C)
            ffn_down(C - 1, 0)
            ffn_down(C - 1, 1)

        @block.vector
        def _(dve):
            v = nc.vector

            def statistics(src, link):
                for t in range(TC):
                    last = v.bn_stats(st6[:, t, :], src(t))
                link(last, apart=True)
                for t in range(TC):
                    last = v.bn_aggr(mv[:, t, :], st6[:, t, :])
                return last

            def normalise(dst, src, t):
                return v.tensor_scalar(dst, src, mv[:, t, 0:1], rstd[:, t:t + 1], ALU.subtract, ALU.mult)

            def layer_norm1(c, b, loads, links):
                link = linker(dve, dve1, links)
                wait_apart(dve, x_in[b], loads * 16)
                statistics(lambda t: x_sb[:, bass.ds(c * TC + t, 1), :], link).then_inc(stats_ready, 1)
                dve.wait_ge(std_ready, c + 1)
                link(v.reciprocal(rstd[:, :], std[:, :]))
                dve.wait_ge(xT_filled, c * KD)
                for t in range(TC):
                    last = normalise(xn[:, t, :], x_sb[:, bass.ds(c * TC + t, 1), :], t)
                last.then_inc(xn_ready, 1)

            def split(c, links):
                for n0 in range(0, SPLITS, 2):
                    pair = (n0, n0 + 1)
                    for n in pair:
                        dve.wait_ge(qk_evacuated, SPLITS + c * SPLITS + n + 1)
                        dve.wait_ge(parts_stored[n], (c + 1) * 16)
                        v.tensor_copy(parts[:, n, 0, :], qf[:, n, :]).then_inc(dve1, 1)
                    for n in pair:
                        dve.wait_ge(dve1, links + n + 1)
                        dve.wait_ge(parts_ready, c * SPLITS + n + 1)
                        v.tensor_tensor(rf[:, n % 2, :], qf[:, n, :], parts[:, n, 0, :], ALU.subtract).then_inc(qf_free, 1)
                    for n in pair:
                        dve.wait_ge(qf_free, SPLITS + c * SPLITS + n + 1)
                        v.tensor_copy(parts[:, n, 1, :], rf[:, n % 2, :]).then_inc(p2_ready, 1)

            def add_v_bias(c):
                for h in range(2):
                    dve.wait_ge(v_filled, c * 2 + h + 1)
                    v.tensor_tensor(v_sb[:, bass.ds(c * TC + 2 * h, 2), :],
                                    bank(6 + h).rearrange("p (t n) -> p t n", t=2), bv_b[:, :, :],
                                    ALU.add).then_inc(v_evacuated, 1)

            def chunk1(c, b, it, last=False):
                links = c * (LN1_LINKS + SPLIT_LINKS) + LN1_LINKS
                if not last:
                    layer_norm1(c + 1, 1 - b, it + 1 + b, links)
                split(c, links if last else links + LN1_LINKS)
                add_v_bias(c)

            for n in range(SPLITS):
                dve.sem_inc(parts_stored[n], 16)
            dve.sem_inc(parts_ready, 2)
            dve.sem_inc(out_stored, 16)
            layer_norm1(0, 0, 1, 0)
            dve.wait_ge(w_in, LOADS * 16)
            v.tensor_scalar(bqs_t[:, :], bq_t[:, :], SCALE, None, ALU.mult).then_inc(bias_scaled, 1)
            with dve.Fori(0, C // 2 - 1) as it:
                for b in range(2):
                    chunk1(it * 2 + b, b, it)
            chunk1(C - 2, 0, C // 2 - 1)
            chunk1(C - 1, 1, C // 2 - 1, last=True)

            def row_max(n, at, i, us, maxed):
                c = i // TC
                if i % TC == 0 and us[0] == 0:
                    dve.wait_ge(negm_ready, maxed)
                dve.wait_ge(ring_filled, n)
                v.tensor_reduce(mx[:, c % 2, i % TC, us[0] // 2:us[0] // 2 + 1],
                                ps[:, at:at + 2, :].rearrange("p a n -> p (a n)")[:, 0:sum(max_cols(i, u) for u in us)],
                                axis=AX.X, op=ALU.max).then_inc(ring_read, 1)

            def chunk_max(n, c):
                dve.wait_ge(ring_read, n)
                v.tensor_reduce(negm[:, c % 2, :], mx[:, c % 2, :, 0:(c + 2) // 2], axis=AX.X, op=ALU.max,
                                negate=True).then_inc(negm_ready, 1)

            def split_shift(n, at, sent, maxed, c):
                rows = bank(at)[0:TC, 0:P]
                dve.wait_ge(ring_filled, n)
                dve.wait_ge(shift_in[c % 2], sent)
                v.tensor_copy(shift[:, c % 2, 0, :], rows).then_inc(shift_hi, 1)
                dve.wait_ge(shift_hi, maxed)
                v.tensor_tensor(shift[:, c % 2, 1, :], rows, shift[:, c % 2, 0, :], ALU.subtract).then_inc(ring_read, 1)

            def add_sums(n, at, ended, c):
                dve.wait_ge(ring_filled, n)
                dve.wait_ge(attn_written, ended)
                sums = bank(at).rearrange("p (t k d) -> p t d k", t=TC, k=4)
                v.tensor_reduce(osum[:, c % 2, :, :], sums[:, :, 0:HD + 1, :], axis=AX.X,
                                op=ALU.add).then_inc(ring_read, 1)
                dve.wait_ge(ring_read, n)
                v.reciprocal(rden[:, c % 2, :], osum[:, c % 2, :, HD]).then_inc(rden_ready, 1)

            maxed = turned = 0
            for what, n, at, _, *args in EARLY:
                if what == "max":
                    _, i, us = args
                    row_max(n, at, i, us, maxed)
                    if i % TC == TC - 1 and us[-1] == i // TC:
                        chunk_max(n, i // TC)
                        maxed += 1
                if what == "shift":
                    split_shift(n, at, turned // 2 * 32, turned + 1, args[1])
                    turned += 1
            EARLY_MAXED = maxed
            with dve.Fori(0, H // HEADS_IN_BODY) as it:
                entries = it * BODY_ENTRIES + EARLY_ENTRIES
                chunks = it * (HEADS_IN_BODY * C)
                maxed, turned, ended = EARLY_MAXED, EARLY_CHUNKS, 0
                for what, *args in BODY:
                    if what not in ("max", "shift", "sums"):
                        continue
                    n, at, _, *args = args
                    if what == "max":
                        _, i, us = args
                        row_max(entries + n, at, i, us, chunks + maxed)
                        if i % TC == TC - 1 and us[-1] == i // TC:
                            chunk_max(entries + n, i // TC)
                            maxed += 1
                    if what == "shift":
                        sent = it * (HEADS_IN_BODY * C * 16) + turned // 2 * 32
                        split_shift(entries + n, at, sent, chunks + (turned + 1), args[1])
                        turned += 1
                    if what == "sums":
                        ended += 1
                        add_sums(entries + n, at, chunks + ended, args[0])

            def add_bias3(bank0, bias, dst, filled, evacuated, c):
                for h in range(2):
                    dve.wait_ge(filled, c * 2 + h + 1)
                    v.tensor_tensor(dst[:, 2 * h:2 * h + 2, :], bank(bank0 + h).rearrange("p (t n) -> p t n", t=2),
                                    bias[:, :, :], ALU.add).then_inc(evacuated, 1)
                wait_apart(dve, evacuated, 2 + c * 2 + 2)

            def standard3(src, link, n):
                statistics(src, link).then_inc(stats3, 1)
                dve.wait_ge(std3, n)
                link(v.reciprocal(rstd[:, :], std[:, :]))

            def attention_branch(c, norms, links):
                link = linker(dve, dve3, links)
                add_bias3(2, bo_b, y, y_filled, y_evacuated, c)
                standard3(lambda t: y[:, t, :], link, norms + 1)
                for t in range(TC):
                    last = normalise(y[:, t, :], y[:, t, :], t)
                link(last)
                link(v.tensor_tensor(tiles(x_sb, c), tiles(x_sb, c), y[:, :, :], ALU.add), apart=True)
                standard3(lambda t: x_sb[:, bass.ds(c * TC + t, 1), :], link, norms + 2)
                for t in range(TC):
                    last = normalise(xn2[:, t, :], x_sb[:, bass.ds(c * TC + t, 1), :], t)
                last.then_inc(xn2_ready, 1)

            def finish(c, norms, links):
                link = linker(dve, dve3, links)
                dve.wait_ge(out_stored, (c + 1) * 16)
                add_bias3(6, b2_b, y2, y2_filled, y2_evacuated, c)
                standard3(lambda t: y2[:, t, :], link, norms + 1)
                for t in range(TC):
                    last = normalise(y2[:, t, :], y2[:, t, :], t)
                link(last)
                v.tensor_tensor(y2[:, :, :], y2[:, :, :], tiles(x_sb, c), ALU.add).then_inc(out_ready, 1)

            dve.wait_ge(w3_in, LOADS3 * 16)
            attention_branch(0, 0, 0)
            with dve.Fori(0, C - 1) as c:
                links = c * (LN3_LINKS + FINISH_LINKS) + LN3_LINKS
                attention_branch(c + 1, c * 3 + 2, links)
                finish(c, c * 3 + 4, links + LN3_LINKS)
            finish(C - 1, 3 * C - 1, (C - 1) * (LN3_LINKS + FINISH_LINKS) + LN3_LINKS)


_INS = ["x", "Wq", "bq", "Wk", "bk", "Wv", "bv", "Wo", "bo", "W1", "b1", "W2", "b2"]
_NAMES = [f"L0_attn_{n}" for n in _INS[:9]] + [f"L0_ffn_{n}" for n in _INS[9:]]


def kernel(**inputs):
    import numpy as _np
    import concourse.bacc as _bacc
    from concourse import mybir as _mybir
    from concourse.bass_utils import run_bass_kernel_spmd as _run

    nc = _bacc.Bacc("TRN2", target_bir_lowering=False, num_devices=1)
    arrays, args = {}, []
    for name in _NAMES:
        a = _np.ascontiguousarray(inputs[name])
        arrays[f"in_{name}"] = a
        args.append(nc.dram_tensor(f"in_{name}", a.shape, _mybir.dt.from_np(a.dtype), kind="ExternalInput").ap())
    out = nc.dram_tensor("out_dram", arrays["in_L0_attn_x"].shape, _mybir.dt.float32, kind="ExternalOutput").ap()
    sandwich_block_kernel(nc, *args, out)
    r = _run(nc, [arrays], core_ids=[0])
    return r.results[0]["out_dram"]
```

```python
import concourse.bass as bass
from concourse import mybir
from contextlib import ExitStack



def sandwich_block_kernel(nc, x, Wq, bq, Wk, bk, Wv, bv, Wo, bo, W1, b1, W2, b2, out):
    fp32, bf16, fp32r = mybir.dt.float32, mybir.dt.bfloat16, mybir.dt.float32r
    ALU, ACT, AX = mybir.AluOpType, mybir.ActivationFunctionType, mybir.AxisListType

    P = 128
    _, S, D = x.shape
    F = W1.shape[1]
    H = 16
    HD = D // H
    SCALE = float(HD) ** -0.5
    EPS = 1e-5
    NEG = -1e30
    CH = 512
    C = S // CH
    T = S // P
    TC = CH // P
    KD = D // P
    KF = F // P

    PARTS = 3
    PAIRS = 6 * HD
    AUG = PAIRS + 2

    QUADS = [(c, jq) for c in range(C) for jq in range(c + 1)]
    NQ = len(QUADS)
    ENTRIES = [(i, list(range(u, min(u + 2, i // TC + 1)))) for i in range(T) for u in range(0, i // TC + 1, 2)]
    LEAD = 11
    LEAD_SLACK = 2
    EARLY_COUNT = [sum(len(us) for _, us in ENTRIES[:n]) for n in range(len(ENTRIES))].index(4 * LEAD)
    HEADS_IN_BODY = 4
    STEPS = HEADS_IN_BODY * NQ
    QUADS_IN_RING = 3
    RING = 4 * QUADS_IN_RING
    RING_BANKS = 5
    EXP_BANKS = 2
    ACC_BANK = RING_BANKS + EXP_BANKS
    H_BANKS = 2
    STACK_DMAS = 9
    VH_STEP = 22

    def exp_cols(c, j):
        return max(0, (j - TC * c)) * P

    def max_cols(i, u):
        return CH if u < i // TC else (i % TC + 1) * P

    class Plan:

        SYNC = 190
        NEAR = 60

        def __init__(self):
            self.pe = self.dve = self.act = self.pool = 0.0
            self.ring = [0.0] * RING_BANKS
            self.exp = [0.0] * EXP_BANKS
            self.acc = 0.0
            self.product = [0.0] * QUADS_IN_RING
            self.last = [0] * RING_BANKS

        def rested(self, n):
            return min(range(RING_BANKS - n + 1), key=lambda b: max(self.ring[b:b + n]))

        def enter(self, kind, at, n, *what):
            self.entries += 1
            need = max(self.last[at:at + n])
            self.last[at:at + n] = [self.entries] * n
            self.order.append((kind, self.entries, at, need, *what))

        def run(self, start, count, exp_side=True):
            self.order, self.entries = [], 0
            st = k = product = issued = 0
            units = 4 * LEAD if exp_side else 0
            turns, ready = [], {}
            while True:
                options = {}
                if exp_side and st < STEPS and st < product + QUADS_IN_RING and units >= 4 * (st + LEAD - LEAD_SLACK):
                    options["exp"] = self.exp[(4 * st + k) % EXP_BANKS]
                if issued < count and (not exp_side or units <= 4 * (min(st, STEPS - 1) + LEAD + LEAD_SLACK)):
                    hb, e = divmod(start + issued, len(ENTRIES))
                    i, us = ENTRIES[e]
                    at = self.rested(len(us))
                    options["max"] = max(self.ring[at:at + len(us)])
                if turns:
                    options[turns[0][0]] = max(turns[0][1], min(self.ring))
                if product < st:
                    c, jq = QUADS[product % NQ]
                    options["values"] = max(ready[product], self.acc if jq == 0 else 0)
                if not options:
                    return self.order
                usable = [x for x in ("shift", "sums", "exp", "max", "values")
                          if x in options and options[x] + self.SYNC <= self.pe + self.NEAR]
                if "values" in usable and st - product >= 2:
                    kind = "values"
                else:
                    kind = usable[0] if usable else min(options, key=options.get)
                self.pe = max(self.pe, options[kind] + self.SYNC)
                if kind == "exp":
                    c, jq = QUADS[st % NQ]
                    cols = CH - exp_cols(c, 4 * jq + k)
                    self.pe += cols / 2.4 + 3
                    if k == 0:
                        self.act = max(self.act, self.product[st % QUADS_IN_RING] + self.SYNC)
                    self.act = max(self.act, self.pe + self.SYNC) + cols / 1.2 + 52
                    self.exp[(4 * st + k) % EXP_BANKS] = ready[st] = self.act
                    if jq == c:
                        self.pool = ready[st] = max(self.pool, self.act + self.SYNC) + 244
                    self.order.append(("exp", st, k))
                    st, k = (st + 1, 0) if k == 3 else (st, k + 1)
                if kind == "max":
                    cols = sum(max_cols(i, u) for u in us)
                    self.pe += cols / 2.4 + 3 * len(us) + (56 if us[-1] == i // TC else 0)
                    self.dve = max(self.dve, self.pe + self.SYNC) + cols / 0.96 + 64
                    self.ring[at:at + len(us)] = [self.dve] * len(us)
                    self.enter("max", at, len(us), hb % HEADS_IN_BODY, i, us)
                    issued += 1
                    units += len(us)
                    if i % TC == TC - 1 and us[-1] == i // TC:
                        self.dve += self.SYNC + 85
                        turns.append(("shift", self.dve, hb % HEADS_IN_BODY, i // TC))
                if kind in ("shift", "sums"):
                    at = self.rested(1)
                    self.pe += {"shift": 107, "sums": 275}[kind]
                    self.dve = max(self.dve, self.pe + self.SYNC) + {"shift": 590, "sums": 348}[kind]
                    self.ring[at] = self.dve
                    self.dve += {"shift": 0, "sums": self.SYNC + 94}[kind]
                    self.enter(kind, at, 1, *turns.pop(0)[2:])
                if kind == "values":
                    self.pe += 4 * (320 if jq == c and c else CH) / 2.4 + 61
                    self.product[product % QUADS_IN_RING] = self.pe
                    self.order.append(("values", product))
                    product += 1
                    if jq == c:
                        self.acc = self.act = max(self.act, self.pe + self.SYNC) + 478
                        self.order.append(("copy", c))
                        turns.append(("sums", self.acc, c))

    plan = Plan()
    EARLY = plan.run(0, EARLY_COUNT, exp_side=False)
    EARLY_ENTRIES = plan.entries
    before = [n - EARLY_ENTRIES for n in plan.last]
    for settling in range(4):
        plan.last = list(before)
        BODY = plan.run(EARLY_COUNT, HEADS_IN_BODY * len(ENTRIES))
        BODY_ENTRIES = plan.entries
        before = [max(b, n - BODY_ENTRIES) for b, n in zip(before, plan.last)]
    assert all(b >= n - BODY_ENTRIES for b, n in zip(before, plan.last))
    EARLY_CHUNKS = sum(x[0] == "shift" for x in EARLY)

    ctx = ExitStack()
    with ctx:
        def sb(name, shape, dt=fp32, life=ctx):
            return life.enter_context(nc.sbuf_tensor(name, shape, dt))

        def sem(name):
            return ctx.enter_context(nc.semaphore(name))

        identf = sb("identf", [P, P])
        identb = sb("identb", [P, P], bf16)
        causal_neg = sb("causal_neg", [P, P], bf16)
        eps_t = sb("eps_t", [P, 1])
        bq_t = sb("bq_t", [P, KD])
        bqs_t = sb("bqs_t", [P, KD])
        bk_t = sb("bk_t", [P, KD])
        bv_b = sb("bv_b", [P, D])
        bo_b = sb("bo_b", [P, D])
        b2_b = sb("b2_b", [P, D])
        b1_t = sb("b1_t", [P, KF])
        st6 = sb("st6", [P, TC, 6])
        mv = sb("mv", [P, TC, 2])
        std = sb("std", [P, TC])
        rstd = sb("rstd", [P, TC])
        mx = sb("mx", [P, 2, TC, 4])
        negm = sb("negm", [P, 2, TC])
        shift = sb("shift", [TC, 2, 2, P], bf16)
        osum = sb("osum", [P, 2, TC, HD + 1])
        rden = sb("rden", [P, 2, TC])
        x_sb = sb("x_sb", [P, T, D])
        attn_sb = sb("attn_sb", [P, T, D])
        wqkv = attn_sb[:, 0:3 * KD, :].rearrange("p (w k) n -> p w k n", w=3)
        WT = [3 * KD + n for n in (0, KD, KD + KD * F // D, KD + KD * F // D + KF)]
        wo_t, w1_t, w2_t = (attn_sb[:, a:b, :].rearrange("p t n -> p (t n)") for a, b in zip(WT, WT[1:]))

        with ExitStack() as phase1:
            xn = sb("xn", [P, TC, D], life=phase1)
            xT_raw = sb("xT_raw", [P, KD, CH], life=phase1)
            xT_hi, xT_lo = (sb(f"xT_{half}", [P, 2, KD, CH], fp32r, phase1) for half in ("hi", "lo"))
            w_hi, w_lo = (sb(f"w_{half}", [P, 3, KD, D], fp32r, phase1) for half in ("hi", "lo"))
        wo_hi, wo_lo = (sb(f"wo_{half}", [P, KD, D], fp32r) for half in ("hi", "lo"))
        w1_hi, w1_lo = (sb(f"w1_{half}", [P, KD, F], fp32r) for half in ("hi", "lo"))
        w2_hi, w2_lo = (sb(f"w2_{half}", [P, KF, D], fp32r) for half in ("hi", "lo"))

        with ExitStack() as attention:
            v_sb = sb("v_sb", [P, T, D], life=attention)
            prob = sb("prob", [P, RING, CH], life=attention)
            acc_s = sb("acc_s", [P, 2, CH], life=attention)
            vh = [sb(f"vh{b}", [P, T, 32], life=attention) for b in range(2)]
            ks = [sb(f"ks{b}", [AUG, S], bf16, life=attention) for b in range(2)]
            qs = [sb(f"qs{b}", [AUG, S], bf16, life=attention) for b in range(2)]
        SPLITS = 2 * KD
        qf, rf = prob[:, 0:SPLITS, :], prob[:, SPLITS:SPLITS + 2, :]
        parts = prob[:, SPLITS + 2:SPLITS + 2 + SPLITS * PARTS // 2, :].rearrange("p a n -> p (a n)").bitcast(
            bf16).rearrange("p (b s n) -> p b s n", b=SPLITS, s=PARTS)

        y, xn2, y2 = (sb(name, [P, TC, D]) for name in ("y", "xn2", "y2"))
        attn_c = sb("attn_c", [P, TC, D])
        row_hi, row_lo = (sb(f"row_{half}", [P, KD, CH], fp32r) for half in ("hi", "lo"))
        xn2T_hi, xn2T_lo = (sb(f"xn2T_{half}", [P, KD, CH], fp32r) for half in ("hi", "lo"))
        H_RAW = 4
        h_raw = sb("h_raw", [P, H_RAW, CH])
        h_hi, h_lo = (sb(f"h_{half}", [P, KF, CH], fp32r) for half in ("hi", "lo"))

        ps = ctx.enter_context(nc.psum_tensor("ps", [P, 8, CH], fp32))

        def bank(n):
            return ps[:, n, :]

        EXP_BANK = RING_BANKS

        scratch = nc.dram_tensor("qk_parts", [2, PARTS, D, S], bf16, kind="Internal").ap()

        const_ready = sem("const_ready")
        w_in = sem("w_in")
        w3_in = sem("w3_in")
        x_in = [sem(f"x_in{b}") for b in range(2)]
        bias_scaled = sem("bias_scaled")
        stats_ready = sem("stats_ready")
        std_ready = sem("std_ready")
        xn_ready = sem("xn_ready")
        xT_filled = sem("xT_filled")
        xT_copied = sem("xT_copied")
        xT_low = sem("xT_low")
        w_high = sem("w_high")
        w_low = sem("w_low")
        qk_filled = sem("qk_filled")
        qk_evacuated = sem("qk_evacuated")
        qf_free = sem("qf_free")
        p2_ready = sem("p2_ready")
        parts_ready = sem("parts_ready")
        parts_stored = [sem(f"parts_stored{n}") for n in range(SPLITS)]
        v_filled = sem("v_filled")
        v_evacuated = sem("v_evacuated")
        dve1 = sem("dve1")
        first_stack_in = sem("first_stack_in")
        stack_in = [sem(f"stack_in{b}") for b in range(2)]
        vh_ready = sem("vh_ready")
        ring_filled = sem("ring_filled")
        ring_read = sem("ring_read")
        negm_ready = sem("negm_ready")
        shift_hi = sem("shift_hi")
        shift_in = [sem(f"shift_in{b}") for b in range(2)]
        scores_filled = sem("scores_filled")
        exp_done = sem("exp_done")
        mask_done = sem("mask_done")
        pv_done = sem("pv_done")
        acc_copied = sem("acc_copied")
        rden_ready = sem("rden_ready")
        attn_written = sem("attn_written")
        attn_c_ready = sem("attn_c_ready")
        t3_filled = sem("t3_filled")
        t3_copied = sem("t3_copied")
        t3_low = sem("t3_low")
        w3_hi = sem("w3_hi")
        w3_ready = sem("w3_ready")
        h_low = sem("h_low")
        y_filled = sem("y_filled")
        y_evacuated = sem("y_evacuated")
        stats3 = sem("stats3")
        std3 = sem("std3")
        xn2_ready = sem("xn2_ready")
        h_filled = sem("h_filled")
        h_ready = sem("h_ready")
        y2_filled = sem("y2_filled")
        y2_evacuated = sem("y2_evacuated")
        dve3 = sem("dve3")
        out_ready = sem("out_ready")
        out_stored = sem("out_stored")

        def wait_apart(eng, s, value):
            value = value if isinstance(value, int) else eng.to_reg(value)
            eng.wait_ge(const_ready, FIRST_CONSTS)
            eng.wait_ge(s, value)

        def linker(eng, s, base):
            n = [0]

            def link(ins, apart=False):
                n[0] += 1
                ins.then_inc(s, 1)
                if apart:
                    wait_apart(eng, s, base + n[0])
                else:
                    eng.wait_ge(s, base + n[0])

            return link

        def head_after(it, hb):
            n = it * HEADS_IN_BODY + (hb + 1)
            return n if hb + 1 < HEADS_IN_BODY else n % H

        def tiles(t, c, n=TC):
            return t[:, bass.ds(c * TC, n), :]

        def twice(bias):
            return bias[:, :].unsqueeze(1).broadcast_to([P, 2, D])

        def f32(t):
            return t.bitcast(fp32)

        x_v = x.rearrange("o (t p) d -> p (o t) d", p=P)
        out_v = out.rearrange("o (t p) d -> p (o t) d", p=P)

        FIRST_CONSTS, CONSTS = 3, 13
        LOADS = 6
        LOADS3 = 6
        LN1_LINKS = 2
        LN3_LINKS, FINISH_LINKS = 6, 3
        block = ctx.enter_context(nc.Block())

        @block.sync
        def _(sp):
            def load_x(c, b):
                sp.dma_start(tiles(x_sb, c), tiles(x_v, c)).then_inc(x_in[b], 16)

            def store_parts(c):
                for n in range(SPLITS):
                    sp.wait_ge(parts_ready, 2 + c * SPLITS + n + 1)
                    dst = scratch[n // KD, :, (n % KD) * P:(n % KD + 1) * P, bass.ds(c * CH, CH)]
                    sp.dma_start(dst.rearrange("s p n -> p s n"), parts[:, n]).then_inc(parts_stored[n], 16)

            load_x(0, 0)
            load_x(1, 1)
            with sp.Fori(0, C // 2 - 1) as it:
                for b in range(2):
                    sp.wait_ge(x_in[b], (it + 1) * 16)
                    load_x(it * 2 + b + 2, b)
                    store_parts(it * 2 + b)

            def load_stack(h, b, loaded, first=0, end=C):
                row, cols = 0, slice(first * CH, end * CH)
                for n in (3, 2, 1):
                    part = 3 - n
                    qsrc = scratch[0, 0:n, bass.ds(h * HD, HD), cols]
                    sp.dma_start(qs[b][row:row + n * HD, cols], qsrc).then_inc(loaded, 16)
                    for r in range(n):
                        ksrc = scratch[1, part, bass.ds(h * HD, HD), cols]
                        sp.dma_start(ks[b][row + r * HD:row + (r + 1) * HD, cols], ksrc).then_inc(loaded, 16)
                    row += n * HD

            def send_shift(n, hb, c):
                sp.wait_ge(ring_read, n)
                dst = qs[hb % 2][PAIRS:AUG, c * CH:(c + 1) * CH].rearrange("s (t n) -> s t n", t=TC)
                for s in range(2):
                    sp.dma_start(dst[s:s + 1], shift[:, c % 2, s, :]).then_inc(shift_in[c % 2], 16)

            for first, end in ((0, C - 2), (C - 2, C)):
                for c in range(max(first, C - 2), end):
                    store_parts(c)
                for n in range(SPLITS):
                    sp.wait_ge(parts_stored[n], 16 + end * 16)
                load_stack(0, 0, stack_in[0] if first else first_stack_in, first, end)
            for what, entry, *rest in EARLY:
                if what == "shift":
                    send_shift(entry, *rest[2:])
            with sp.Fori(0, H // HEADS_IN_BODY) as it:
                entries = it * BODY_ENTRIES + EARLY_ENTRIES
                for what, *args in BODY:
                    if what == "exp" and args[0] % NQ == 1 and args[1] == 0:
                        hb = args[0] // NQ
                        sp.wait_ge(exp_done, EXP_BANKS + it * (4 * STEPS) + 4 * NQ * hb)
                        load_stack(head_after(it, hb), (hb + 1) % 2, stack_in[(hb + 1) % 2])
                    if what == "shift":
                        entry, _, _, hb, c = args
                        send_shift(entries + entry, hb, c)

            with sp.Fori(0, C) as c:
                sp.wait_ge(out_ready, c + 1)
                sp.dma_start(tiles(out_v, c), y2[:, :, :]).then_inc(out_stored, 16)
            sp.wait_ge(out_stored, 16 + C * 16)
            for b in range(2):
                sp.wait_ge(shift_in[b], (H * C + EARLY_CHUNKS) // 2 * 32)
                sp.wait_ge(stack_in[b], (H // 2 + 1 - b) * STACK_DMAS * 16)

        @block.gpsimd
        def _(pool):
            g = nc.gpsimd
            made = [0]

            def constant(ins):
                made[0] += 1
                ins.then_inc(const_ready, 1)
                pool.wait_ge(const_ready, made[0])

            constant(g.memset(eps_t[:, :], EPS))

            def identity(m):
                constant(g.memset(m[:, :], 0.0))
                constant(g.affine_select(out=m[:, :], in_=m[:, :], compare_op=ALU.not_equal, fill=1.0, base=0,
                                         pattern=[[-1, P]], channel_multiplier=1))

            identity(identf)
            assert made[0] == FIRST_CONSTS
            identity(identb)
            constant(g.memset(causal_neg[:, :], 0.0))
            constant(g.affine_select(out=causal_neg[:, :], in_=causal_neg[:, :], compare_op=ALU.is_ge, fill=NEG,
                                     base=0, pattern=[[-1, P]], channel_multiplier=1))
            for b in range(2):
                constant(g.memset(ks[b][PAIRS:AUG, :], 1.0))
                constant(g.memset(vh[b][:, :, :], 0.0))
                constant(g.memset(vh[b][:, :, HD:HD + 1], 1.0))
            assert made[0] == CONSTS

            def low_xT(c, b):
                for k in range(KD):
                    pool.wait_ge(xT_copied, c * KD + k + 1)
                    g.tensor_tensor(xT_lo[:, b, k, :], xT_raw[:, k, :], f32(xT_hi[:, b, k, :]),
                                    ALU.subtract).then_inc(xT_low, 1)

            def third_parts(c, ns):
                for n in ns:
                    pool.wait_ge(p2_ready, c * SPLITS + n + 1)
                    g.tensor_tensor(parts[:, n, 2, :], rf[:, n % 2, :], parts[:, n, 1, :],
                                    ALU.subtract).then_inc(parts_ready, 1)

            def chunk1(c, b, last=False):
                third_parts(c, range(2))
                if not last:
                    low_xT(c + 1, 1 - b)
                third_parts(c, range(2, SPLITS))

            low_xT(0, 0)
            with pool.Fori(0, C // 2 - 1) as it:
                for b in range(2):
                    chunk1(it * 2 + b, b)
            chunk1(C - 2, 0)
            chunk1(C - 1, 1, last=True)

            def lay_out_values(h, b):
                g.tensor_copy(vh[b][:, :, 0:HD], v_sb[:, :, bass.ds(h * HD, HD)]).then_inc(vh_ready, 1)

            pool.wait_ge(v_evacuated, 2 + 2 * C)
            lay_out_values(0, 0)

            for n, (hi, lo, w) in enumerate(((wo_hi, wo_lo, wo_t), (w1_hi, w1_lo, w1_t), (w2_hi, w2_lo, w2_t))):
                pool.wait_ge(w3_hi, n + 1)
                g.tensor_tensor(lo.rearrange("p k n -> p (k n)"), w, f32(hi.rearrange("p k n -> p (k n)")),
                                ALU.subtract).then_inc(w3_ready, 1)

            def scale_out(n, c, h):
                pool.wait_ge(rden_ready, n)
                g.tensor_tensor(attn_sb[:, c * TC:(c + 1) * TC, bass.ds(h * HD, HD)],
                                osum[:, c % 2, :, 0:HD],
                                rden[:, c % 2, :].unsqueeze(2).broadcast_to([P, TC, HD]),
                                ALU.mult).then_inc(attn_written, 1)

            def mask_diagonal(tiles_before, st, c):
                for k in range(4):
                    n = 4 * st + k
                    wait_apart(pool, exp_done, tiles_before + (EXP_BANKS + n + 1))
                    if c == 0 and k > 0:
                        g.memset(prob[:, n % RING, 0:k * P], 0.0)
                    g.affine_select(out=prob[:, n % RING, k * P:(k + 1) * P],
                                    in_=prob[:, n % RING, k * P:(k + 1) * P],
                                    compare_op=ALU.is_ge, fill=0.0, base=0,
                                    pattern=[[1, P]], channel_multiplier=-1).then_inc(mask_done, 1)

            with pool.Fori(0, H // HEADS_IN_BODY) as it:
                quads = it * STEPS
                chunks = it * (HEADS_IN_BODY * C)
                ended = 0
                for what, *args in BODY:
                    if what == "exp" and args[1] == 3:
                        st = args[0]
                        hb, (c, jq) = st // NQ, QUADS[st % NQ]
                        if st % NQ == VH_STEP:
                            pool.wait_ge(pv_done, QUADS_IN_RING + quads + NQ * hb)
                            lay_out_values(head_after(it, hb), (hb + 1) % 2)
                        if jq == c:
                            mask_diagonal(quads * 4, st, c)
                    if what == "sums":
                        ended += 1
                        scale_out(chunks + ended, args[3], it * HEADS_IN_BODY + (ended - 1) // C)

            def low_hidden(c):
                for f in range(KF):
                    pool.wait_ge(h_ready, H_BANKS + c * KF + f + 1)
                    g.tensor_tensor(h_lo[:, f, :], h_raw[:, f % H_RAW, :], f32(h_hi[:, f, :]),
                                    ALU.subtract).then_inc(h_low, 1)

            pool.wait_ge(attn_written, 2 + H * C)
            with pool.Fori(0, C - 2) as c:
                pool.wait_ge(t3_filled, c * 4 + 4)
                g.tensor_copy(attn_c[:, :, :], tiles(attn_sb, c + 2)).then_inc(attn_c_ready, 1)
                low_hidden(c)
            low_hidden(C - 2)
            low_hidden(C - 1)

        @block.scalar
        def _(act):
            for n, w in enumerate((Wq, Wk, Wv)):
                act.dma_start(wqkv[:, n], w.rearrange("(k p) n -> p k n", p=P)).then_inc(w_in, 16)
            act.dma_start(bq_t[:, :], bq.rearrange("(m p) -> p m", p=P), allow_slow_non_contiguous=True).then_inc(w_in, 16)
            act.dma_start(bk_t[:, :], bk.rearrange("(m p) -> p m", p=P), allow_slow_non_contiguous=True).then_inc(w_in, 16)

            act.dma_start(bv_b[:, :], bv.partition_broadcast(P)).then_inc(w_in, 16)

            def deviation(c):
                act.wait_ge(stats_ready, c + 1)
                nc.scalar.activation(std[:, :], mv[:, :, 1], ACT.Sqrt, bias=eps_t[:, 0:1]).then_inc(std_ready, 1)

            def copy_xT(c, b):
                for k in range(KD):
                    act.wait_ge(xT_filled, c * KD + k + 1)
                    act.wait_ge(xT_low, c * KD + k + 1)
                    nc.scalar.activation(xT_raw[:, k, :], bank(k), ACT.Copy)
                    nc.scalar.activation(xT_hi[:, b, k, :], bank(k), ACT.Copy).then_inc(xT_copied, 1)

            def evacuate_qk(c):
                for n in range(SPLITS):
                    act.wait_ge(qk_filled, c * SPLITS + n + 1)
                    act.wait_ge(qf_free, c * SPLITS + n + 1)
                    act.wait_ge(parts_stored[n], (c + 1) * 16)
                    bias, scale = (bqs_t, bk_t)[n // KD][:, n % KD:n % KD + 1], (SCALE, 1.0)[n // KD]
                    nc.scalar.activation(qf[:, n, :], bank(2 + n), ACT.Identity, bias=bias, scale=scale)
                    nc.scalar.activation(parts[:, n, 0, :], bank(2 + n), ACT.Identity, bias=bias,
                                         scale=scale).then_inc(qk_evacuated, 1)

            act.wait_ge(const_ready, FIRST_CONSTS)
            deviation(0)
            act.wait_ge(w_in, LOADS * 16)
            nc.scalar.activation(w_hi[:, :, :, :], wqkv, ACT.Copy).then_inc(w_high, 1)
            copy_xT(0, 0)
            for dst, w in ((wo_t, Wo), (w1_t, W1), (w2_t, W2)):
                n = w.shape[1]
                act.dma_start(dst.rearrange("p (k n) -> p k n", n=n), w.rearrange("(k p) n -> p k n", p=P)).then_inc(w3_in, 16)
            act.dma_start(bo_b[:, :], bo.partition_broadcast(P)).then_inc(w3_in, 16)
            act.dma_start(b2_b[:, :], b2.partition_broadcast(P)).then_inc(w3_in, 16)
            act.dma_start(b1_t[:, :], b1.rearrange("(m p) -> p m", p=P), allow_slow_non_contiguous=True).then_inc(w3_in, 16)
            act.wait_ge(bias_scaled, 1)

            def chunk1(c, b, last=False):
                if not last:
                    deviation(c + 1)
                evacuate_qk(c)
                if not last:
                    copy_xT(c + 1, 1 - b)

            with act.Fori(0, C // 2 - 1) as it:
                for b in range(2):
                    chunk1(it * 2 + b, b)
            chunk1(C - 2, 0)
            chunk1(C - 1, 1, last=True)

            act.wait_ge(w3_in, LOADS3 * 16)
            act.wait_ge(v_filled, 2 * C)
            for hi, w in ((wo_hi, wo_t), (w1_hi, w1_t), (w2_hi, w2_t)):
                nc.scalar.activation(hi.rearrange("p k n -> p (k n)"), w, ACT.Copy).then_inc(w3_hi, 1)

            def copy_acc(c):
                nc.scalar.activation(acc_s[:, c % 2, :], bank(ACC_BANK), ACT.Copy).then_inc(acc_copied, 1)

            with act.Fori(0, H // HEADS_IN_BODY) as it:
                quads = it * STEPS
                for what, *args in BODY:
                    if what == "exp":
                        st, k = args
                        c, jq = QUADS[st % NQ]
                        if k == 0:
                            act.wait_ge(pv_done, quads + (st + 1))
                        col = exp_cols(c, 4 * jq + k)
                        act.wait_ge(scores_filled, quads * 4 + (4 * st + k + 1))
                        nc.scalar.activation(prob[:, (4 * st + k) % RING, col:CH],
                                             bank(EXP_BANK + (4 * st + k) % EXP_BANKS)[:, col:CH], ACT.Exp).then_inc(exp_done, 1)
                    if what == "values":
                        product = args[0]
                    if what == "copy":
                        act.wait_ge(pv_done, QUADS_IN_RING + quads + (product + 1))
                        copy_acc(args[0])

            def copy_T3(before, dst):
                for k in range(KD):
                    act.wait_ge(t3_filled, before + (k + 1))
                    nc.scalar.activation(dst[:, k, :], bank(k), ACT.Copy).then_inc(t3_copied, 1)

            def deviation3(n):
                act.wait_ge(stats3, n)
                nc.scalar.activation(std[:, :], mv[:, :, 1], ACT.Sqrt, bias=eps_t[:, 0:1]).then_inc(std3, 1)

            def relu(c, f):
                act.wait_ge(h_filled, c * KF + f + 1)
                act.wait_ge(h_low, c * KF + f + 1)
                nc.scalar.activation(h_raw[:, f % H_RAW, :], bank(4 + f % 2), ACT.Relu, bias=b1_t[:, f:f + 1])
                nc.scalar.activation(h_hi[:, f, :], bank(4 + f % 2), ACT.Relu,
                                     bias=b1_t[:, f:f + 1]).then_inc(h_ready, 1)

            copy_T3(0, row_hi)
            copy_T3(KD, row_hi)
            deviation3(1)
            deviation3(2)
            copy_T3(2 * KD, xn2T_hi)

            def chunk3(c, last=False):
                for f in range(KF):
                    if f == 4:
                        deviation3(c * 3 + 3)
                    relu(c, f)
                deviation3(c * 3 + 4)
                if not last:
                    copy_T3(c * 4 + 6, row_hi)
                copy_T3(c * 4 + (6 if last else 8), xn2T_hi)
                deviation3(c * 3 + 5)

            with act.Fori(0, C - 2) as c:
                chunk3(c)
            chunk3(C - 2, last=True)
            for f in range(KF):
                relu(C - 1, f)
            deviation3(3 * C)

        @block.tensor
        def _(pe):
            mm, tr = nc.tensor.matmul, nc.tensor.transpose

            def transpose_x(c):
                pe.wait_ge(xn_ready, c + 1)
                if not (isinstance(c, int) and c == 0):
                    pe.wait_ge(xT_copied, c * KD)
                for k in range(KD):
                    for t in range(TC):
                        last = tr(bank(k)[:, t * P:(t + 1) * P], xn[:, t, k * P:(k + 1) * P], identf[:, :])
                    last.then_inc(xT_filled, 1)

            def project_qk(c, b):
                pe.wait_ge(xT_copied, c * KD + KD)

                def products(n, operands, begins, ends):
                    passes = [(w, x, k) for w, x in operands for k in range(KD)]
                    for i, (w, x, k) in enumerate(passes):
                        last = mm(bank(2 + n), w[:, n // KD, k, (n % KD) * P:(n % KD + 1) * P], x[:, b, k, :],
                                  start=(begins and i == 0), stop=(ends and i == len(passes) - 1))
                    return last

                for n0 in range(0, SPLITS, 2):
                    for n in (n0, n0 + 1):
                        pe.wait_ge(qk_evacuated, c * SPLITS + n + 1)
                        products(n, ((w_hi, xT_hi), (w_lo, xT_hi)), True, False)
                    if n0 == 0:
                        pe.wait_ge(xT_low, KD + c * KD + KD)
                    for n in (n0, n0 + 1):
                        products(n, ((w_hi, xT_lo),), False, True).then_inc(qk_filled, 1)

            def project_v(c, b):
                for h in range(2):
                    pe.wait_ge(v_evacuated, c * 2 + h + 1)
                    for t in (2 * h, 2 * h + 1):
                        passes = [(x, w, k) for x, w in ((xT_hi, w_hi), (xT_hi, w_lo), (xT_lo, w_hi))
                                  for k in range(KD)]
                        for n, (x, w, k) in enumerate(passes):
                            last = mm(bank(6 + h)[:, (t % 2) * D:(t % 2 + 1) * D], x[:, b, k, t * P:(t + 1) * P],
                                      w[:, 2, k, :], start=(n == 0), stop=(n == len(passes) - 1))
                    last.then_inc(v_filled, 1)

            def chunk1(c, b, last=False):
                project_qk(c, b)
                if not last:
                    transpose_x(c + 1)
                project_v(c, b)

            pe.sem_inc(qk_evacuated, SPLITS)
            pe.sem_inc(qf_free, SPLITS)
            pe.sem_inc(xT_low, KD)
            pe.sem_inc(v_evacuated, 2)
            pe.wait_ge(const_ready, FIRST_CONSTS)
            transpose_x(0)
            pe.wait_ge(w_high, 1)
            pe.wait_ge(w_low, 1)
            with pe.Fori(0, C // 2 - 1) as it:
                for b in range(2):
                    chunk1(it * 2 + b, b)
            chunk1(C - 2, 0)
            chunk1(C - 1, 1, last=True)

            def score_max(at, need, hb, i, us):
                if need is not None:
                    pe.wait_ge(ring_read, need)
                for u in us:
                    dst, cols, diag = bank(at + u - us[0]), max_cols(i, u), u == i // TC
                    last = mm(dst[:, 0:cols], qs[hb % 2][0:PAIRS, i * P:(i + 1) * P], ks[hb % 2][0:PAIRS, u * CH:u * CH + cols],
                              start=True, stop=not diag)
                    if diag:
                        last = mm(dst[:, cols - P:cols], identb[:, :], causal_neg[:, :], start=False, stop=True)
                last.then_inc(ring_filled, 1)

            def turn_shift(at, need, maxed, c):
                pe.wait_ge(negm_ready, maxed)
                pe.wait_ge(ring_read, need)
                tr(bank(at)[0:TC, 0:P], negm[:, c % 2, :], identf[:, :]).then_inc(ring_filled, 1)

            def turn_sums(at, need, copied, c):
                pe.wait_ge(acc_copied, 1 + copied)
                pe.wait_ge(ring_read, need)
                for t in range(TC):
                    last = tr(bank(at)[:, t * P:(t + 1) * P], acc_s[:, c % 2, t * P:(t + 1) * P], identf[:, :])
                last.then_inc(ring_filled, 1)

            def values(st, it):
                hb, (c, jq) = st // NQ, QUADS[st % NQ]
                if jq == 0:
                    pe.wait_ge(acc_copied, it * (HEADS_IN_BODY * C) + (hb * C + c + 1))
                if c == 0:
                    pe.wait_ge(vh_ready, it * HEADS_IN_BODY + (hb + 1))
                pe.wait_ge(exp_done, it * (4 * STEPS) + (EXP_BANKS + 4 * st + 4))
                if jq == c:
                    pe.wait_ge(mask_done, it * (HEADS_IN_BODY * C * 4) + 4 * (hb * C + c + 1))
                for k in range(4):
                    j = 4 * jq + k
                    col = exp_cols(c, j) if c else 0
                    last = mm(bank(ACC_BANK)[32 * k:32 * k + 32, col:CH], vh[hb % 2][:, j, :],
                              prob[:, (4 * st + k) % RING, col:CH], start=(jq == 0), stop=(jq == c))
                last.then_inc(pv_done, 1)

            pe.sem_inc(exp_done, EXP_BANKS)
            pe.sem_inc(pv_done, QUADS_IN_RING)
            pe.sem_inc(acc_copied, 1)
            pe.sem_inc(attn_written, 2)
            pe.wait_ge(const_ready, CONSTS)
            pe.wait_ge(qk_evacuated, SPLITS + C * SPLITS)
            pe.wait_ge(xT_copied, KD * C)
            pe.wait_ge(first_stack_in, STACK_DMAS * 16)
            maxed = 0
            for what, _, at, need, *args in EARLY:
                if what == "max":
                    score_max(at, need if need > 0 else None, *args)
                if what == "shift":
                    maxed += 1
                    turn_shift(at, need, maxed, args[1])
            pe.wait_ge(stack_in[0], STACK_DMAS * 16)
            pe.wait_ge(v_evacuated, 2 + 2 * C)
            with pe.Fori(0, H // HEADS_IN_BODY) as it:
                entries = it * BODY_ENTRIES + EARLY_ENTRIES
                chunks = it * (HEADS_IN_BODY * C)
                maxed, copied = EARLY_CHUNKS, 0
                for what, *args in BODY:
                    if what == "exp":
                        st, k = args
                        hb, (c, jq) = st // NQ, QUADS[st % NQ]
                        if jq == 0 and k == 0:
                            pe.wait_ge(shift_in[c % 2], (it * (HEADS_IN_BODY * C // 2) + (hb * (C // 2) + c // 2 + 1)) * 32)
                        j, col = 4 * jq + k, exp_cols(c, 4 * jq + k)
                        pe.wait_ge(exp_done, it * (4 * STEPS) + (4 * st + k + 1))
                        mm(bank(EXP_BANK + (4 * st + k) % EXP_BANKS)[:, col:CH], ks[hb % 2][0:AUG, j * P:(j + 1) * P],
                           qs[hb % 2][0:AUG, c * CH + col:(c + 1) * CH], start=True, stop=True).then_inc(scores_filled, 1)
                    if what == "max":
                        _, at, need, hb, i, us = args
                        if (i, us[0]) == (0, 0):
                            loads = it * (HEADS_IN_BODY // 2) + ((hb or HEADS_IN_BODY) // 2 + 1)
                            pe.wait_ge(stack_in[hb % 2], loads * (STACK_DMAS * 16))
                        score_max(at, entries + need, hb, i, us)
                    if what == "shift":
                        maxed += 1
                        _, at, need, hb, c = args
                        turn_shift(at, entries + need, chunks + maxed, c)
                    if what == "sums":
                        copied += 1
                        _, at, need, c = args
                        turn_sums(at, entries + need, chunks + copied, c)
                    if what == "values":
                        values(args[0], it)

            def turn(src):
                for k in range(KD):
                    for t in range(TC):
                        last = tr(bank(k)[:, t * P:(t + 1) * P], src[:, t, k * P:(k + 1) * P], identf[:, :])
                    last.then_inc(t3_filled, 1)

            def attend_out(c):
                pe.wait_ge(t3_low, c * 4 if not isinstance(c, int) or c else KD)
                pe.wait_ge(y_evacuated, c * 2 + 2)
                for t in range(TC):
                    passes = [(a, b, k) for a, b in ((row_hi, wo_hi), (row_hi, wo_lo), (row_lo, wo_hi))
                              for k in range(KD)]
                    for n, (a, b, k) in enumerate(passes):
                        last = mm(bank(2 + t // 2)[:, (t % 2) * D:(t % 2 + 1) * D], a[:, k, t * P:(t + 1) * P],
                                  b[:, k, :], start=(n == 0), stop=(n == len(passes) - 1))
                    if t % 2:
                        last.then_inc(y_filled, 1)

            def ffn_up(c, copied):
                pe.wait_ge(t3_low, copied)
                for f in range(KF):
                    pe.wait_ge(h_ready, c * KF + f + 1)
                    passes = [(a, b, k) for a, b in ((w1_hi, xn2T_hi), (w1_lo, xn2T_hi), (w1_hi, xn2T_lo))
                              for k in range(KD)]
                    for n, (a, b, k) in enumerate(passes):
                        last = mm(bank(4 + f % 2), a[:, k, f * P:(f + 1) * P], b[:, k, :],
                                  start=(n == 0), stop=(n == len(passes) - 1))
                    last.then_inc(h_filled, 1)

            def ffn_down(c, h):
                pe.wait_ge(y2_evacuated, c * 2 + h + 1)
                for t in (2 * h, 2 * h + 1):
                    passes = [(h_hi, b, f) for f in range(KF) for b in (w2_hi, w2_lo)]
                    passes += [(h_lo, w2_hi, f) for f in range(KF)]
                    for n, (a, b, f) in enumerate(passes):
                        if t == 0 and b is w2_hi:
                            if a is h_hi:
                                pe.wait_ge(h_ready, H_BANKS + c * KF + f + 1)
                            else:
                                pe.wait_ge(h_low, H_RAW + c * KF + f + 1)
                        last = mm(bank(6 + h)[:, (t % 2) * D:(t % 2 + 1) * D], a[:, f, t * P:(t + 1) * P],
                                  b[:, f, :], start=(n == 0), stop=(n == len(passes) - 1))
                last.then_inc(y2_filled, 1)

            def chunk3(c, last=False):
                ffn_up(c, c * 4 + 6)
                if not last:
                    pe.wait_ge(attn_c_ready, c + 1)
                    turn(attn_c)
                ffn_down(c, 0)
                pe.wait_ge(xn2_ready, c + 2)
                pe.wait_ge(t3_low, c * 4 + (6 if last else 8))
                turn(xn2)
                ffn_down(c, 1)
                if not last:
                    attend_out(c + 2)

            pe.sem_inc(h_ready, H_BANKS)
            pe.sem_inc(h_low, H_RAW)
            pe.sem_inc(y_evacuated, 2)
            pe.sem_inc(y2_evacuated, 2)
            pe.wait_ge(w3_ready, 3)
            pe.wait_ge(ring_read, H // HEADS_IN_BODY * BODY_ENTRIES + EARLY_ENTRIES)
            pe.wait_ge(attn_written, 2 + (H - 1) * C + 2)
            turn(attn_sb[:, 0:TC, :])
            attend_out(0)
            turn(attn_sb[:, TC:2 * TC, :])
            attend_out(1)
            pe.wait_ge(xn2_ready, 1)
            pe.wait_ge(t3_low, 2 * KD)
            turn(xn2)
            with pe.Fori(0, C - 2) as c:
                chunk3(c)
            chunk3(C - 2, last=True)
            ffn_up(C - 1, 4 * C)
            ffn_down(C - 1, 0)
            ffn_down(C - 1, 1)

        @block.vector
        def _(dve):
            v = nc.vector

            def statistics(src, link):
                for t in range(TC):
                    last = v.bn_stats(st6[:, t, :], src(t))
                link(last, apart=True)
                for t in range(TC):
                    last = v.bn_aggr(mv[:, t, :], st6[:, t, :])
                return last

            def normalise(dst, src, t):
                return v.tensor_scalar(dst, src, mv[:, t, 0:1], rstd[:, t:t + 1], ALU.subtract, ALU.mult)

            def layer_norm1(c, b, loads, links):
                link = linker(dve, dve1, links)
                wait_apart(dve, x_in[b], loads * 16)
                statistics(lambda t: x_sb[:, bass.ds(c * TC + t, 1), :], link).then_inc(stats_ready, 1)
                dve.wait_ge(std_ready, c + 1)
                link(v.reciprocal(rstd[:, :], std[:, :]))
                dve.wait_ge(xT_filled, c * KD)
                for t in range(TC):
                    last = normalise(xn[:, t, :], x_sb[:, bass.ds(c * TC + t, 1), :], t)
                last.then_inc(xn_ready, 1)

            def split(c):
                for n0 in range(0, SPLITS, 2):
                    pair = (n0, n0 + 1)
                    for n in pair:
                        dve.wait_ge(qk_evacuated, SPLITS + c * SPLITS + n + 1)
                        dve.wait_ge(parts_ready, c * SPLITS + n + 1)
                        v.tensor_tensor(rf[:, n % 2, :], qf[:, n, :], parts[:, n, 0, :], ALU.subtract).then_inc(qf_free, 1)
                    for n in pair:
                        dve.wait_ge(qf_free, SPLITS + c * SPLITS + n + 1)
                        v.tensor_copy(parts[:, n, 1, :], rf[:, n % 2, :]).then_inc(p2_ready, 1)

            def add_v_bias(c):
                for h in range(2):
                    dve.wait_ge(v_filled, c * 2 + h + 1)
                    v.tensor_tensor(v_sb[:, bass.ds(c * TC + 2 * h, 2), :],
                                    bank(6 + h).rearrange("p (t n) -> p t n", t=2), twice(bv_b),
                                    ALU.add).then_inc(v_evacuated, 1)

            def chunk1(c, b, it, last=False):
                links = c * LN1_LINKS + LN1_LINKS
                if not last:
                    layer_norm1(c + 1, 1 - b, it + 1 + b, links)
                split(c)
                add_v_bias(c)

            for n in range(SPLITS):
                dve.sem_inc(parts_stored[n], 16)
            dve.sem_inc(parts_ready, 2)
            dve.sem_inc(out_stored, 16)
            layer_norm1(0, 0, 1, 0)
            dve.wait_ge(w_in, LOADS * 16)
            dve.wait_ge(w_high, 1)
            v.tensor_tensor(w_lo[:, :, :, :], wqkv, f32(w_hi[:, :, :, :]), ALU.subtract).then_inc(w_low, 1)
            v.tensor_scalar(bqs_t[:, :], bq_t[:, :], SCALE, None, ALU.mult).then_inc(bias_scaled, 1)
            with dve.Fori(0, C // 2 - 1) as it:
                for b in range(2):
                    chunk1(it * 2 + b, b, it)
            chunk1(C - 2, 0, C // 2 - 1)
            chunk1(C - 1, 1, C // 2 - 1, last=True)

            def row_max(n, at, i, us, maxed):
                c = i // TC
                if i % TC == 0 and us[0] == 0:
                    dve.wait_ge(negm_ready, maxed)
                dve.wait_ge(ring_filled, n)
                v.tensor_reduce(mx[:, c % 2, i % TC, us[0] // 2:us[0] // 2 + 1],
                                ps[:, at:at + 2, :].rearrange("p a n -> p (a n)")[:, 0:sum(max_cols(i, u) for u in us)],
                                axis=AX.X, op=ALU.max).then_inc(ring_read, 1)

            def chunk_max(n, c):
                dve.wait_ge(ring_read, n)
                v.tensor_reduce(negm[:, c % 2, :], mx[:, c % 2, :, 0:(c + 2) // 2], axis=AX.X, op=ALU.max,
                                negate=True).then_inc(negm_ready, 1)

            def split_shift(n, at, sent, maxed, c):
                rows = bank(at)[0:TC, 0:P]
                dve.wait_ge(ring_filled, n)
                dve.wait_ge(shift_in[c % 2], sent)
                v.tensor_copy(shift[:, c % 2, 0, :], rows).then_inc(shift_hi, 1)
                dve.wait_ge(shift_hi, maxed)
                v.tensor_tensor(shift[:, c % 2, 1, :], rows, shift[:, c % 2, 0, :], ALU.subtract).then_inc(ring_read, 1)

            def add_sums(n, at, ended, c):
                dve.wait_ge(ring_filled, n)
                dve.wait_ge(attn_written, ended)
                sums = bank(at).rearrange("p (t k d) -> p t d k", t=TC, k=4)
                v.tensor_reduce(osum[:, c % 2, :, :], sums[:, :, 0:HD + 1, :], axis=AX.X,
                                op=ALU.add).then_inc(ring_read, 1)
                dve.wait_ge(ring_read, n)
                v.reciprocal(rden[:, c % 2, :], osum[:, c % 2, :, HD]).then_inc(rden_ready, 1)

            maxed = turned = 0
            for what, n, at, _, *args in EARLY:
                if what == "max":
                    _, i, us = args
                    row_max(n, at, i, us, maxed)
                    if i % TC == TC - 1 and us[-1] == i // TC:
                        chunk_max(n, i // TC)
                        maxed += 1
                if what == "shift":
                    split_shift(n, at, turned // 2 * 32, turned + 1, args[1])
                    turned += 1
            EARLY_MAXED = maxed
            with dve.Fori(0, H // HEADS_IN_BODY) as it:
                entries = it * BODY_ENTRIES + EARLY_ENTRIES
                chunks = it * (HEADS_IN_BODY * C)
                maxed, turned, ended = EARLY_MAXED, EARLY_CHUNKS, 0
                for what, *args in BODY:
                    if what not in ("max", "shift", "sums"):
                        continue
                    n, at, _, *args = args
                    if what == "max":
                        _, i, us = args
                        row_max(entries + n, at, i, us, chunks + maxed)
                        if i % TC == TC - 1 and us[-1] == i // TC:
                            chunk_max(entries + n, i // TC)
                            maxed += 1
                    if what == "shift":
                        sent = it * (HEADS_IN_BODY * C * 16) + turned // 2 * 32
                        split_shift(entries + n, at, sent, chunks + (turned + 1), args[1])
                        turned += 1
                    if what == "sums":
                        ended += 1
                        add_sums(entries + n, at, chunks + ended, args[0])

            def add_bias3(bank0, bias, dst, filled, evacuated, c):
                for h in range(2):
                    dve.wait_ge(filled, c * 2 + h + 1)
                    v.tensor_tensor(dst[:, 2 * h:2 * h + 2, :], bank(bank0 + h).rearrange("p (t n) -> p t n", t=2),
                                    twice(bias), ALU.add).then_inc(evacuated, 1)
                wait_apart(dve, evacuated, 2 + c * 2 + 2)

            def standard3(src, link, n):
                statistics(src, link).then_inc(stats3, 1)
                dve.wait_ge(std3, n)
                link(v.reciprocal(rstd[:, :], std[:, :]))

            def attention_branch(c, norms, links):
                link = linker(dve, dve3, links)
                add_bias3(2, bo_b, y, y_filled, y_evacuated, c)
                standard3(lambda t: y[:, t, :], link, norms + 1)
                for t in range(TC):
                    last = normalise(y[:, t, :], y[:, t, :], t)
                link(last)
                link(v.tensor_tensor(tiles(x_sb, c), tiles(x_sb, c), y[:, :, :], ALU.add), apart=True)
                standard3(lambda t: x_sb[:, bass.ds(c * TC + t, 1), :], link, norms + 2)
                for t in range(TC):
                    last = normalise(xn2[:, t, :], x_sb[:, bass.ds(c * TC + t, 1), :], t)
                last.then_inc(xn2_ready, 1)

            def finish(c, norms, links):
                link = linker(dve, dve3, links)
                dve.wait_ge(out_stored, (c + 1) * 16)
                add_bias3(6, b2_b, y2, y2_filled, y2_evacuated, c)
                standard3(lambda t: y2[:, t, :], link, norms + 1)
                for t in range(TC):
                    last = normalise(y2[:, t, :], y2[:, t, :], t)
                link(last)
                v.tensor_tensor(y2[:, :, :], y2[:, :, :], tiles(x_sb, c), ALU.add).then_inc(out_ready, 1)

            def low_T3(before, hi, lo):
                for k in range(KD):
                    dve.wait_ge(t3_copied, before + (k + 1))
                    v.tensor_tensor(lo[:, k, :], bank(k), f32(hi[:, k, :]), ALU.subtract).then_inc(t3_low, 1)

            dve.wait_ge(w3_in, LOADS3 * 16)
            low_T3(0, row_hi, row_lo)
            low_T3(KD, row_hi, row_lo)
            attention_branch(0, 0, 0)
            low_T3(2 * KD, xn2T_hi, xn2T_lo)

            def chunk3(c, last=False):
                links = c * (LN3_LINKS + FINISH_LINKS) + LN3_LINKS
                attention_branch(c + 1, c * 3 + 2, links)
                if not last:
                    low_T3(c * 4 + 6, row_hi, row_lo)
                low_T3(c * 4 + (6 if last else 8), xn2T_hi, xn2T_lo)
                finish(c, c * 3 + 4, links + LN3_LINKS)

            with dve.Fori(0, C - 2) as c:
                chunk3(c)
            chunk3(C - 2, last=True)
            finish(C - 1, 3 * C - 1, (C - 1) * (LN3_LINKS + FINISH_LINKS) + LN3_LINKS)


_INS = ["x", "Wq", "bq", "Wk", "bk", "Wv", "bv", "Wo", "bo", "W1", "b1", "W2", "b2"]
_NAMES = [f"L0_attn_{n}" for n in _INS[:9]] + [f"L0_ffn_{n}" for n in _INS[9:]]


def kernel(**inputs):
    import numpy as _np
    import concourse.bacc as _bacc
    from concourse import mybir as _mybir
    from concourse.bass_utils import run_bass_kernel_spmd as _run

    nc = _bacc.Bacc("TRN2", target_bir_lowering=False, num_devices=1)
    arrays, args = {}, []
    for name in _NAMES:
        a = _np.ascontiguousarray(inputs[name])
        arrays[f"in_{name}"] = a
        args.append(nc.dram_tensor(f"in_{name}", a.shape, _mybir.dt.from_np(a.dtype), kind="ExternalInput").ap())
    out = nc.dram_tensor("out_dram", arrays["in_L0_attn_x"].shape, _mybir.dt.float32, kind="ExternalOutput").ap()
    sandwich_block_kernel(nc, *args, out)
    r = _run(nc, [arrays], core_ids=[0])
    return r.results[0]["out_dram"]
```
